# Optimizing a Trainium2 kernel written in Bass

```python
import numpy as np
import jax
import jax.numpy as jnp

def _softmax(x, axis=-1):
    return jax.nn.softmax(x, axis=axis)

def _gelu(x):
    return jax.nn.gelu(x, approximate=True)

def _silu(x):
    return jax.nn.silu(x)

def _sigmoid(x):
    return jax.nn.sigmoid(x)

def _layernorm(x, axis=-1, eps=1e-05):
    m = jnp.mean(x, axis=axis, keepdims=True)
    v = jnp.var(x, axis=axis, keepdims=True)
    return (x - m) / jnp.sqrt(v + eps)

def _scatter_add(tgt, idx, src, axis=0):
    return tgt.at[idx].add(src)

def _segment_sum(src, seg, n):
    return jax.ops.segment_sum(src, seg, n)
kernel_name = 'mk_gnn_resnorm_d4_gnn_r8_4bbdc7'

def setup_inputs(seed: int=0):
    np.random.seed(seed)
    _w = jnp.asarray

    def _rec_inputs():
        import jax
        import jax.numpy as jnp
        _gk = jax.random.key(seed)
        x = -0.0003713 + 1 * jax.random.normal(jax.random.fold_in(_gk, 1), (12500, 128), jnp.float32)
        _s = jax.random.randint(jax.random.fold_in(_gk, 2), (100000,), 0, 12500, jnp.int32)
        _d = jax.random.randint(jax.random.fold_in(_gk, 3), (100000,), 0, 12500, jnp.int32)
        _loop = jnp.arange(12500, dtype=jnp.int32)
        src = jnp.concatenate([_s, _d, _loop])
        dst = jnp.concatenate([_d, _s, _loop])
        _o = jnp.argsort(dst, stable=True)
        src = src[_o]
        dst = dst[_o]
        edge_attr_128 = -8.513e-05 + 0.999844 * jax.random.normal(jax.random.fold_in(_gk, 12), (212500, 128), jnp.float32)
        edge_weight1 = jax.random.uniform(jax.random.fold_in(_gk, 14), (212500, 1), jnp.float32, 0.0, 0.999998)
        return (x, src, dst, edge_attr_128, edge_weight1)
    x, src, dst, edge_attr_128, edge_weight1 = _rec_inputs()

    def _L0_gnn_setup():
        import jax, jax.numpy as jnp
        import numpy as np
        N_NODES = 12500
        N_EDGES = 200000
        F_IN = 128
        UNITS = 128
        key = jax.random.key(seed)
        k1, k2, k3, k4, k5, k6 = jax.random.split(key, 6)
        node_features = jax.random.normal(k1, (N_NODES, F_IN), dtype=jnp.float32)
        edge_row = jax.random.randint(k2, (N_EDGES,), 0, N_NODES, dtype=jnp.int32)
        edge_col = jax.random.randint(k3, (N_EDGES,), 0, N_NODES, dtype=jnp.int32)
        s_t = 1.0 / np.sqrt(F_IN)
        s_u = 1.0 / np.sqrt(F_IN + UNITS)
        W_t = jax.random.uniform(k4, (F_IN, UNITS), minval=-s_t, maxval=s_t, dtype=jnp.float32)
        W_u = jax.random.uniform(k5, (F_IN + UNITS, UNITS), minval=-s_u, maxval=s_u, dtype=jnp.float32)
        b_u = jnp.zeros((UNITS,), dtype=jnp.float32)
        return {'node_features': node_features, 'W_t': W_t, 'W_u': W_u, 'b_u': b_u, 'edge_row': edge_row, 'edge_col': edge_col}
    _L0_gnn_all = _L0_gnn_setup()
    _L0_gnn_in = {k: v for k, v in _L0_gnn_all.items() if k in ('W_t', 'W_u', 'b_u')}
    del _L0_gnn_all

    def _L1_gnn_setup():
        import jax, jax.numpy as jnp
        import numpy as np
        N_NODES = 12500
        N_EDGES = 200000
        D_FEAT = 128
        key = jax.random.key(seed)
        k1, k2 = jax.random.split(key)
        x = jax.random.normal(k1, (N_NODES, D_FEAT), dtype=jnp.float32)
        eps = jnp.zeros((1,), dtype=jnp.float32)
        edge_index = jax.random.randint(k2, (2, N_EDGES), 0, N_NODES, dtype=jnp.int64)
        return {'x': x, 'eps': eps, 'edge_index': edge_index}
    _L1_gnn_all = _L1_gnn_setup()
    _L1_gnn_in = {k: v for k, v in _L1_gnn_all.items() if k in ('eps',)}
    del _L1_gnn_all

    def _L2_gnn_setup():
        import jax, jax.numpy as jnp
        import numpy as np
        N_NODES = 6250
        N_EDGES = 100000
        D = 128
        key = jax.random.key(seed)
        ks = jax.random.split(key, 8)
        n_feat = jax.random.normal(ks[0], (N_NODES, D), dtype=jnp.float32)
        e_feat = jax.random.normal(ks[1], (N_EDGES, 1), dtype=jnp.float32)
        edge_weight = jax.random.uniform(ks[2], (N_EDGES, 1), dtype=jnp.float32)
        src = jax.random.randint(ks[3], (N_EDGES,), 0, N_NODES)
        dst = jax.random.randint(ks[4], (N_EDGES,), 0, N_NODES)
        eps = jnp.zeros((1,), dtype=jnp.float32)
        W1 = jax.random.normal(ks[5], (D, D), dtype=jnp.float32) * 0.05
        b1 = jnp.zeros((D,), dtype=jnp.float32)
        W2 = jax.random.normal(ks[6], (D, D), dtype=jnp.float32) * 0.05
        b2 = jnp.zeros((D,), dtype=jnp.float32)
        return {'n_feat': n_feat, 'e_feat': e_feat, 'edge_weight': edge_weight, 'src': src, 'dst': dst, 'eps': eps, 'W1': W1, 'b1': b1, 'W2': W2, 'b2': b2}
    _L2_gnn_all = _L2_gnn_setup()
    _L2_gnn_in = {k: v for k, v in _L2_gnn_all.items() if k in ('eps', 'W1', 'b1', 'W2', 'b2')}
    del _L2_gnn_all

    def _L3_gnn_setup():
        import jax, jax.numpy as jnp
        import numpy as np
        N, E, D, G, H, O = (1250, 80000, 128, 128, 512, 128)

        def mish(x):
            return x * jnp.tanh(jax.nn.softplus(x))
        key = jax.random.key(seed)
        ks = jax.random.split(key, 10)
        nodes = jax.random.normal(ks[0], (N, D), dtype=jnp.float32)
        edges = jax.random.normal(ks[1], (E, D), dtype=jnp.float32)
        globals_g = jax.random.normal(ks[2], (1, G), dtype=jnp.float32)
        senders = jax.random.randint(ks[3], (E,), 0, N)
        receivers = jax.random.randint(ks[4], (E,), 0, N)
        lim_e = np.sqrt(6.0 / (D + D)).astype(np.float32)
        W_e_k = jax.random.uniform(ks[5], (D, D), jnp.float32, -lim_e, lim_e)
        W_e_b = jnp.zeros((D,), jnp.float32)
        eps = jnp.zeros((1, 1), jnp.float32)
        lim1 = np.sqrt(6.0 / (D + G + H)).astype(np.float32)
        W1 = jax.random.uniform(ks[6], (D + G, H), jnp.float32, -lim1, lim1)
        b1 = jnp.zeros((H,), jnp.float32)
        lim2 = np.sqrt(6.0 / (H + O)).astype(np.float32)
        W2 = jax.random.uniform(ks[7], (H, O), jnp.float32, -lim2, lim2)
        b2 = jnp.zeros((O,), jnp.float32)
        return {'nodes': nodes, 'edges': edges, 'globals_g': globals_g, 'W_e_k': W_e_k, 'W_e_b': W_e_b, 'eps': eps, 'W1': W1, 'b1': b1, 'W2': W2, 'b2': b2, 'senders': senders, 'receivers': receivers}
    _L3_gnn_all = _L3_gnn_setup()
    _L3_gnn_in = {k: v for k, v in _L3_gnn_all.items() if k in ('globals_g', 'W_e_k', 'W_e_b', 'eps', 'W1', 'b1', 'W2', 'b2')}
    del _L3_gnn_all
    return {'x': x, 'src': src, 'dst': dst, 'edge_attr_128': edge_attr_128, 'edge_weight1': edge_weight1, 'L0_gnn_W_t': _L0_gnn_in['W_t'], 'L0_gnn_W_u': _L0_gnn_in['W_u'], 'L0_gnn_b_u': _L0_gnn_in['b_u'], 'L1_gnn_eps': _L1_gnn_in['eps'], 'L2_gnn_eps': _L2_gnn_in['eps'], 'L2_gnn_W1': _L2_gnn_in['W1'], 'L2_gnn_b1': _L2_gnn_in['b1'], 'L2_gnn_W2': _L2_gnn_in['W2'], 'L2_gnn_b2': _L2_gnn_in['b2'], 'L3_gnn_globals_g': _L3_gnn_in['globals_g'], 'L3_gnn_W_e_k': _L3_gnn_in['W_e_k'], 'L3_gnn_W_e_b': _L3_gnn_in['W_e_b'], 'L3_gnn_eps': _L3_gnn_in['eps'], 'L3_gnn_W1': _L3_gnn_in['W1'], 'L3_gnn_b1': _L3_gnn_in['b1'], 'L3_gnn_W2': _L3_gnn_in['W2'], 'L3_gnn_b2': _L3_gnn_in['b2']}

def reference(x, src, dst, edge_attr_128, edge_weight1, L0_gnn_W_t, L0_gnn_W_u, L0_gnn_b_u, L1_gnn_eps, L2_gnn_eps, L2_gnn_W1, L2_gnn_b1, L2_gnn_W2, L2_gnn_b2, L3_gnn_globals_g, L3_gnn_W_e_k, L3_gnn_W_e_b, L3_gnn_eps, L3_gnn_W1, L3_gnn_b1, L3_gnn_W2, L3_gnn_b2):
    import jax
    import jax.numpy as jnp

    def _L0_gnn_ref(node_features, W_t, W_u, b_u, edge_row, edge_col):
        import jax, jax.numpy as jnp
        import numpy as np
        N_NODES = 12500
        N_EDGES = 200000
        F_IN = 128
        UNITS = 128
        n = node_features.shape[0]
        h = node_features @ W_t
        msgs = h[edge_col]
        agg_sum = jax.ops.segment_sum(msgs, edge_row, num_segments=n)
        deg = jax.ops.segment_sum(jnp.ones_like(edge_row, dtype=h.dtype), edge_row, num_segments=n)
        deg_inv = jnp.where(deg > 0, 1.0 / deg, 0.0)
        agg = agg_sum * deg_inv[:, None]
        cat = jnp.concatenate([node_features, agg], axis=-1)
        return jax.nn.relu(cat @ W_u + b_u)

    def _L1_gnn_ref(x, eps, edge_index):
        import jax, jax.numpy as jnp
        import numpy as np
        N_NODES = 12500
        N_EDGES = 200000
        D_FEAT = 128
        row, col = (edge_index[0], edge_index[1])
        n = x.shape[0]
        deg = jax.ops.segment_sum(jnp.ones(col.shape, dtype=x.dtype), col, num_segments=n)
        deg_inv_sqrt = jnp.where(deg > 0, jax.lax.rsqrt(deg), jnp.zeros_like(deg))
        norm = deg_inv_sqrt[row] * deg_inv_sqrt[col]
        msgs = norm[:, None] * x[col]
        agg = jax.ops.segment_sum(msgs, row, num_segments=n)
        out = agg + (1.0 + eps[0]) * x
        return out

    def _L2_gnn_ref(n_feat, e_feat, edge_weight, src, dst, eps, W1, b1, W2, b2):
        import jax, jax.numpy as jnp
        import numpy as np
        N_NODES = 6250
        N_EDGES = 100000
        D = 128
        msg = n_feat[src] * edge_weight
        neigh = jax.ops.segment_sum(msg, dst, num_segments=n_feat.shape[0])
        rst = (1.0 + eps) * n_feat + neigh
        h = jax.nn.relu(rst @ W1 + b1)
        return h @ W2 + b2

    def _L3_gnn_ref(nodes, edges, globals_g, W_e_k, W_e_b, eps, W1, b1, W2, b2, senders, receivers):
        import jax, jax.numpy as jnp
        import numpy as np
        N, E, D, G, H, O = (1250, 80000, 128, 128, 512, 128)

        def mish(x):
            return x * jnp.tanh(jax.nn.softplus(x))
        n = nodes.shape[0]
        sent = nodes[senders]
        e = mish(sent + edges @ W_e_k + W_e_b)
        agg = jax.ops.segment_sum(e, receivers, num_segments=n)
        h = (1.0 + eps) * nodes + agg
        g = jnp.broadcast_to(globals_g, (n, globals_g.shape[-1]))
        h = jnp.concatenate([h, g], axis=-1)
        h = jax.nn.relu(h @ W1 + b1) @ W2 + b2
        return h
    edge_index = jnp.stack([src, dst])
    x = _layernorm(x + _L0_gnn_ref(x, L0_gnn_W_t, L0_gnn_W_u, L0_gnn_b_u, src, dst), axis=-1)
    x = _layernorm(x + _L1_gnn_ref(x, L1_gnn_eps, edge_index), axis=-1)
    x = _layernorm(x + _L2_gnn_ref(x, edge_weight1, edge_weight1, src, dst, L2_gnn_eps, L2_gnn_W1, L2_gnn_b1, L2_gnn_W2, L2_gnn_b2), axis=-1)
    x = _layernorm(x + _L3_gnn_ref(x, edge_attr_128, L3_gnn_globals_g, L3_gnn_W_e_k, L3_gnn_W_e_b, L3_gnn_eps, L3_gnn_W1, L3_gnn_b1, L3_gnn_W2, L3_gnn_b2, src, dst), axis=-1)
    return x

_drawn_inputs = setup_inputs


def setup_inputs(seed=0):
    import zlib

    import numpy as np

    out = dict(_drawn_inputs(seed))
    spreads = {'L0_gnn_b_u': (0.0, 0.1),
     'L2_gnn_b1': (0.0, 0.297),
     'L2_gnn_b2': (0.0, 0.1),
     'L3_gnn_W_e_b': (0.0, 0.1),
     'L3_gnn_b1': (0.0, 0.409),
     'L3_gnn_b2': (0.0, 0.366)}
    factors = {}
    for name, (base, spread) in spreads.items():
        noise = np.random.default_rng([zlib.crc32(name.encode()), seed]).standard_normal(out[name].shape)
        drawn = base * np.exp(spread * noise) if base else spread * noise
        out[name] = jnp.asarray(drawn.astype(out[name].dtype))
    for name, factor in factors.items():
        out[name] = (out[name] * factor).astype(out[name].dtype)
    return out
```

```python
import concourse.bass as bass
from concourse import mybir
from contextlib import ExitStack, contextmanager

P = 128
T = 128
SE = P * T
W1C = P + 1
SG = 12
NQ = 8
HID = 512
LN_EPS = 1e-5


class Tally:

    def __init__(self, sem):
        self.sem, self.n, self.terms = sem, 0, ()

    def inc(self, k=1):
        self.n += k

    def at(self):
        return self.sem, self.n, self.terms


def wait(e, mark):
    sem, n, terms = mark
    v = n
    for var, per in terms:
        v = var * per + v
    e.wait_ge(sem, v)


@contextmanager
def loop(e, trips, *tallies_per):
    with e.Fori(0, trips) as it:
        start = [(t, t.n, t.terms) for t, _ in tallies_per]
        for t, per in tallies_per:
            t.terms = t.terms + ((it, per),)
        yield it
        for (t, n0, terms), (_, per) in zip(start, tallies_per):
            assert t.n - n0 == per, (t.sem, t.n - n0, per)
            t.n, t.terms = n0 + per * trips, terms


@contextmanager
def count(trips, *tallies_per):
    start = [(t, t.n) for t, _ in tallies_per]
    yield 0
    for (t, n0), (_, per) in zip(start, tallies_per):
        assert t.n - n0 == per, (t.sem, t.n - n0, per)
        t.n = n0 + per * trips


def graph_layers(nc, x_in, src_in, dst_in, edge_in, w_in, Wt, Wu, bu, eps1, eps2, W21, b21, W22, b22,
                 glob, We, be, eps3, W31, b31, W32, b32, out):
    f32, bf16, i32 = mybir.dt.float32, mybir.dt.bfloat16, mybir.dt.int32
    ALU, ACT, AX = mybir.AluOpType, mybir.ActivationFunctionType, mybir.AxisListType
    N, E = x_in.shape[0], src_in.shape[0]
    NB = -(-N // P)
    SUP = -(-E // SE)
    TILES = SUP * T
    K = T + NB - 1
    KI = -(-K // SG)
    KP = KI * SG
    NG = next(g for g in (7, 4, 2, 1) if NB % g == 0)
    GROUPS = NB // NG
    LASTN = N - (NB - 1) * P
    GA = min(4, NG)
    x1, x2, x3 = (nc.dram_tensor(n, (NB * P, P), f32, kind="Internal").ap() for n in ("x1", "x2", "x3"))
    t1, t3 = (nc.dram_tensor(n, (NB * P, P), f32, kind="Internal").ap() for n in ("t1", "t3"))

    with ExitStack() as ctx:
        ctx.enter_context(nc.allow_non_contiguous_dma("index blocks and biases"))

        def sb(name, shape, dt=f32):
            return ctx.enter_context(nc.sbuf_tensor(name, shape, dt))

        def sem(name):
            return ctx.enter_context(nc.semaphore(name))

        M = sb("M", [P, T, W1C])
        acc = sb("acc", [P, NB, W1C])
        acc_flat = acc[:, :, :].rearrange("p a f -> p (a f)")
        M_flat = M[:, :, :].rearrange("p a f -> p (a f)")
        relS, relD = sb("relS", [P, max(SUP * KP + SG, 16 * P)]), sb("relD", [P, SUP * KP + SG])
        tab = sb("tab", [P, SUP * KP], i32)
        gS, gD = sb("gS", [P, max(TILES + NQ, 8 * P)], i32), sb("gD", [P, TILES + NQ], i32)
        perm = sb("perm", [P, TILES + NQ], i32)
        wD = sb("wD", [P, TILES])
        ixb, ixe = sb("ixb", [P, T], i32), sb("ixe", [P, T], i32)
        oh = sb("oh", [P, SG, P])
        ident, ones_f, iota128 = sb("ident", [P, P]), sb("ones_f", [P, P]), sb("iota128", [P, P])
        iotaK, iota_p, neg128p, bigcol = sb("iotaK", [P, KP]), sb("iota_p", [P, 1]), sb("neg128p", [P, 1]), sb("bigcol", [P, 1])
        sbase = sb("sbase", [P, SUP])
        ones_b, ltri, iotaNb = sb("ones_b", [P, P], bf16), sb("ltri", [P, P], bf16), sb("iotaNb", [P, NB], bf16)
        iota128b = sb("iota128b", [P, P], bf16)
        degD = sb("degD", [P, NB])
        eps_sb = sb("eps_sb", [P, 4])
        wtu_sb, wua_sb = sb("wtu_sb", [P, P]), sb("wua_sb", [P, P])
        w21_sb, w22_sb, we_sb = (sb(n, [P, P]) for n in ("w21_sb", "w22_sb", "we_sb"))
        w31_sb, w32_sb = sb("w31_sb", [P, HID]), sb("w32_sb", [P, HID // P, P])
        bias = sb("bias", [P, 4, P])
        b21c, globc, b31c = sb("b21c", [P, 1]), sb("globc", [P, 1]), sb("b31c", [P, HID // P])
        degm = sb("degm", [P, NB])

        arena = [M_flat, 0, T * W1C]

        def take(cols, dt=f32):
            n = cols if dt != bf16 else -(-cols // 2)
            v = arena[0][:, arena[1]:arena[1] + n]
            arena[1] += n
            assert arena[1] <= arena[2]
            return v if dt == f32 else v.bitcast(dt)

        raw_s, raw_d, raw_w = take(TILES, i32), take(TILES, i32), take(TILES)
        gsum, cx = (take(g * NB, bf16).rearrange("p (g b) -> p g b", b=NB) for g in (32, 34))
        t2 = take(32 * 2 * NB, bf16).rearrange("p (g b) -> p g b", b=2 * NB)
        ohl = take(8 * P).rearrange("p (j c) -> p j c", c=P)
        oht = take(8 * 3 * P).rearrange("p (j c) -> p j c", c=3 * P)
        arena[:] = [acc_flat, 0, NB * W1C]
        ohh = take(T * NB, bf16).rearrange("p (t b) -> p t b", b=NB)
        ti = [take(T, i32) for _ in range(3)]
        khi, kf, gf, klo, pos, lane, tile_f = (take(T) for _ in range(7))
        pays = [take(T) for _ in range(3)]
        tot, endp, base_, endt = (take(NB) for _ in range(4))
        cum0, cmp = take(NB, bf16), take(KP, bf16)
        endi, lcol = take(NB, i32), take(2)
        bmin, tau, sel = take(KP), take(KP), take(KP)
        prod = take(8 * NB).rearrange("p (g b) -> p g b", b=NB)
        ohlo = take(8 * P, bf16).rearrange("p (j c) -> p j c", c=P)
        keys, keyT = take(P), take(P)
        er, et = sb("er", [P, NQ, P]), sb("et", [P, 2, 4 * P])
        relS_flat = relS[:, :]
        vb, eb = (relS_flat[:, i * 8 * P:(i + 1) * 8 * P].rearrange("p (g c) -> p g c", g=2) for i in range(2))
        wb = gS[:, 0:8 * P].bitcast(f32).rearrange("p (g c) -> p g c", g=2)
        arena[:] = [M_flat, 0, T * W1C]
        NW = NG * P
        nxg, nag, nxT, naT, nh2, nz, nout = (take(NW) for _ in range(7))
        nhT = take(NW * (HID // P))
        nst, nmv, nrs = take(NG * 6), take(NG * 2), take(NG * 2)
        oh_flat = oh[:, :, :].rearrange("p a f -> p (a f)")
        wt_sb, wub_sb, w31g_sb = oh_flat[:, 0:P], oh_flat[:, P:2 * P], oh_flat[:, 2 * P:2 * P + HID]

        ps = ctx.enter_context(nc.psum_tensor("ps", [P, 8, 512], f32))

        s_ld, s_cst, s_v, s_p, s_a = (sem(n) for n in ("s_ld", "s_cst", "s_v", "s_p", "s_a"))
        s_g = [sem(f"s_g{i}") for i in range(16)]
        s_e = [sem(f"s_e{i}") for i in range(16)]
        s_arr, s_oh, s_st, s_add, s_ix, s_m = (sem(n) for n in ("s_arr", "s_oh", "s_st", "s_add", "s_ix", "s_m"))
        s_tr, s_et, s_u, s_vv, s_ex, s_mv, s_c = (
            sem(n) for n in ("s_tr", "s_et", "s_u", "s_vv", "s_ex", "s_mv", "s_c"))
        s_dum, s_dum_v, s_dum_a, s_dum_s = (sem(n) for n in ("s_dum", "s_dum_v", "s_dum_a", "s_dum_s"))
        s_nl, s_ns, s_nv, s_np, s_na = (sem(n) for n in ("s_nl", "s_ns", "s_nv", "s_np", "s_na"))

        def sort(e, role, tv, tp, key, gat, wts, out_rel, out_g, row):
            V, Q = role == "v", role == "p"
            lp = (lambda trips, *t: loop(e, trips, *t)) if role in "vp" else (lambda trips, *t: count(trips, *t))

            def v(make, *marks, chain=True, gate=False):
                if V:
                    for m in marks:
                        wait(e, m)
                    if chain:
                        wait(e, tv.at())
                    if gate:
                        e.sem_inc(s_dum_v, 1)
                    make().then_inc(s_v, 1)
                tv.inc()

            def p(make, *marks):
                if Q:
                    for m in marks:
                        wait(e, m)
                    make().then_inc(s_p, 1)
                tp.inc()

            npay = 3 if wts is not None else 2
            per_v = (NV_DST if wts is not None else NV_SRC)
            per_p = NP_SORT
            with lp(SUP, (tv, per_v), (tp, per_p)) as s:
                blk = bass.ds(s * T, T) if (V or Q) else slice(0, T)
                v(lambda: e.tensor_scalar(ti[0], key[:, blk], 7, None, ALU.logical_shift_right))
                v(lambda: e.tensor_copy(khi, ti[0]))
                v(lambda: e.tensor_copy(kf, key[:, blk]), gate=True)
                v(lambda: e.tensor_copy(gf, gat[:, blk]), gate=True)
                if wts is None:
                    v(lambda: e.tensor_copy(pays[0], kf))
                    v(lambda: e.tensor_scalar(pays[1], gf, float(N - 1), None, ALU.min))
                else:
                    v(lambda: e.tensor_scalar(gf, gf, float(N - 1), 128.0, ALU.min, ALU.mult))
                    v(lambda: e.tensor_scalar(pays[0], gf, iota_p[:, 0:1], None, ALU.add))
                    v(lambda: e.scalar_tensor_tensor(pays[1], kf, 128.0, iota128[:, :], ALU.mult, ALU.add))
                    v(lambda: e.tensor_copy(pays[2], wts[:, blk]), gate=True)
                    v(lambda: e.tensor_scalar(ti[1], key[:, blk], 127, None, ALU.bitwise_and))
                    v(lambda: e.tensor_copy(klo, ti[1]))
                split = tv.at()
                with lp(T // 8, (tv, 8)) as c:
                    for j in range(8):
                        v(lambda: e.tensor_scalar(ohh[:, bass.ds(c * 8 + j, 1), :].rearrange("p a b -> p (a b)"), iotaNb[:, :],
                                                  khi[:, bass.ds(c * 8 + j, 1)], None, ALU.is_equal),
                          *([split] if j == 0 else []), chain=False)
                oh4 = ohh.rearrange("p (g c) b -> p g (c b)", c=4)
                v(lambda: e.tensor_tensor(t2, oh4[:, :, 0:2 * NB], oh4[:, :, 2 * NB:4 * NB], ALU.add))
                v(lambda: e.tensor_tensor(gsum, t2[:, :, 0:NB], t2[:, :, NB:2 * NB], ALU.add))
                v(lambda: e.memset(cx[:, 0, :], 0.0))
                with lp(32, (tv, 1)) as g:
                    v(lambda: e.tensor_tensor(cx[:, bass.ds(g + 1, 1), :].rearrange("p a b -> p (a b)"),
                                              cx[:, bass.ds(g, 1), :].rearrange("p a b -> p (a b)"),
                                              gsum[:, bass.ds(g, 1), :].rearrange("p a b -> p (a b)"), ALU.add))
                p(lambda: e.matmul(ps[:, 7, 0:NB], ones_b[:, :], cx[:, 32, :], start=True, stop=True), tv.at())
                v(lambda: e.tensor_copy(tot, ps[:, 7, 0:NB]), tp.at())
                v(lambda: e.tensor_tensor_scan(endp, ones_f[:, 0:NB], tot, 0.0, ALU.mult, ALU.add))
                v(lambda: e.tensor_tensor(base_, endp, tot, ALU.subtract))
                v(lambda: e.tensor_scalar(base_, base_, neg128p[:, 0:1], 0.0, ALU.add, ALU.max))
                v(lambda: e.tensor_scalar(cum0, base_, 128.0, None, ALU.min))
                v(lambda: e.tensor_tensor(cx[:, 0:32, :], cx[:, 0:32, :],
                                          cum0.rearrange("p (a b) -> p a b", a=1).to_broadcast([P, 32, NB]), ALU.add))
                biased = tv.at()
                v(lambda: e.tensor_copy(endi, endp))
                v(lambda: e.tensor_scalar(endi, endi, 7, None, ALU.logical_shift_right))
                v(lambda: e.tensor_scalar(endt, endi, T - 1, None, ALU.min))
                v(lambda: e.tensor_tensor(endt, endt, iota128[:, 0:NB], ALU.add))
                v(lambda: e.tensor_tensor(endt, endt, ident[:, 0:NB], ALU.mult))
                v(lambda: e.tensor_reduce(lcol[:, 0:1], endt, AX.X, ALU.add))
                v(lambda: e.tensor_tensor(lcol[:, 1:2], lcol[:, 0:1], bigcol[:, :], ALU.add))
                v(lambda: e.tensor_scalar(cmp, iotaK[:, :], lcol[:, 1:2], None, ALU.is_gt))
                p(lambda: e.matmul(ps[:, 7, 128:128 + KP], ones_b[:, :], cmp, start=True, stop=True), tv.at())
                v(lambda: e.tensor_scalar(bmin, ps[:, 7, 128:128 + KP], float(NB - 1), None, ALU.min), tp.at())
                v(lambda: e.tensor_tensor(tau, iotaK[:, :], bmin, ALU.subtract))
                v(lambda: e.tensor_scalar(tau, tau, float(T - 1), None, ALU.min))
                v(lambda: e.tensor_scalar(sel, tau, iota_p[:, 0:1], None, ALU.is_equal))
                v(lambda: e.memset(sel[:, K:KP], 0.0))
                kb = bass.ds(s * KP, KP) if V else slice(0, KP)
                v(lambda: e.tensor_copy(tab[row:row + 1, kb], tau[row:row + 1, :]), gate=True)
                v(lambda: e.tensor_copy(tab[row + 32:row + 33, kb], bmin[row + 32:row + 33, :]), gate=True)
                v0 = tv.at()
                with lp(16, (tv, 4), (tp, 2)) as h:
                    ranks = []
                    for i in range(2):
                        g = h * 2 + i if (V or Q) else 0
                        o = ps[:, 4 + i, 0:4 * NB].rearrange("p (c b) -> p c b", b=NB)

                        def rank():
                            e.matmul(o, ltri[:, :], ohh[:, bass.ds(g * 4, 4), :], start=True, stop=False)
                            e.matmul(o, ones_b[:, :], cx[:, bass.ds(g, 1), :].to_broadcast([P, 4, NB]), start=False, stop=False)
                            for c in range(3):
                                i_ = e.matmul(o[:, c + 1:4, :], ones_b[:, :],
                                              ohh[:, bass.ds(g * 4 + c, 1), :].to_broadcast([P, 3 - c, NB]),
                                              start=False, stop=c == 2)
                            return i_

                        p(rank, (s_v, tv.n - (2 - 2 * i), tv.terms))
                        ranks.append(tp.at())
                    for i in range(2):
                        g = h * 2 + i if (V or Q) else 0
                        o = ps[:, 4 + i, 0:4 * NB].rearrange("p (c b) -> p c b", b=NB)
                        v(lambda: e.tensor_tensor(prod[:, 4 * i:4 * i + 4, :], o, ohh[:, bass.ds(g * 4, 4), :], ALU.mult), ranks[i])
                        v(lambda: e.tensor_reduce(pos[:, bass.ds(g * 4, 4)], prod[:, 4 * i:4 * i + 4, :], AX.X, ALU.add))
                v(lambda: e.tensor_copy(ti[0], pos))
                v(lambda: e.tensor_scalar(ti[1], ti[0], 127, None, ALU.bitwise_and))
                v(lambda: e.tensor_scalar(ti[2], ti[0], 7, None, ALU.logical_shift_right))
                v(lambda: e.tensor_copy(lane, ti[1]))
                v(lambda: e.tensor_copy(tile_f, ti[2]))
                ready = tv.at()
                nv = 1 + npay + (1 if wts is not None else 0)

                def move(c0, first, last):
                    before = tp.at()
                    for j in range(8):
                        if V:
                            if j == 0:
                                wait(e, ready)
                                wait(e, before)
                            c = bass.ds(c0 + j, 1)
                            e.tensor_scalar(ohl[:, j, :], iota128[:, :], lane[:, c], None, ALU.is_equal)
                            if wts is not None:
                                e.tensor_scalar(ohlo[:, j, :], iota128b[:, :], klo[:, c], None, ALU.is_equal)
                            for i in range(npay):
                                ins = e.tensor_scalar(oht[:, j, i * P:(i + 1) * P], iota128[:, :], tile_f[:, c],
                                                      pays[i][:, c], ALU.is_equal, ALU.mult)
                            ins.then_inc(s_v, 1)
                        tv.inc()

                        def mm():
                            if wts is not None:
                                e.matmul(ps[:, 7, 0:NB], ohlo[:, j, :], ohh[:, bass.ds(c0 + j, 1), :].rearrange("p a b -> p (a b)"),
                                         start=first and j == 0, stop=last and j == 7)
                            return e.matmul(ps[:, 6, 0:npay * P], ohl[:, j, :], oht[:, j, 0:npay * P],
                                            start=first and j == 0, stop=last and j == 7)
                        p(mm, tv.at())

                move(0, True, False)
                with lp(T // 8 - 2, (tv, 8), (tp, 8)) as c:
                    move(c * 8 + 8 if (V or Q) else 0, False, False)
                move(T - 8, False, True)
                moved = tp.at()
                if wts is None:
                    v(lambda: e.tensor_copy(keys, ps[:, 6, 0:P]), moved)
                    v(lambda: e.tensor_copy(out_g[:, blk], ps[:, 6, P:2 * P]), gate=True)
                else:
                    v(lambda: e.tensor_copy(ti[0], ps[:, 6, 0:P]), moved)
                    v(lambda: e.tensor_scalar(out_g[:, blk], ti[0], 7, None, ALU.logical_shift_right))
                    v(lambda: e.tensor_scalar(ti[0], ti[0], 127, None, ALU.bitwise_and))
                    v(lambda: e.tensor_copy(ti[1], ps[:, 6, P:2 * P]))
                    v(lambda: e.tensor_scalar(ti[2], ti[1], 7, None, ALU.logical_shift_right))
                    v(lambda: e.tensor_scalar(ti[1], ti[1], 127, None, ALU.bitwise_and))
                    v(lambda: e.tensor_copy(keys, ti[2]))
                    v(lambda: e.tensor_copy(kf, ti[0]))
                    v(lambda: e.tensor_copy(gf, ti[1]))
                    v(lambda: e.scalar_tensor_tensor(kf, kf, 128.0, gf, ALU.mult, ALU.add))
                    v(lambda: e.tensor_scalar(kf, kf, sbase[:, bass.ds(s, 1)], float(E - 1), ALU.add, ALU.min))
                    v(lambda: e.tensor_copy(perm[:, blk], kf), gate=True)
                    v(lambda: e.tensor_copy(wD[:, blk], ps[:, 6, 2 * P:3 * P]), gate=True)
                    v(lambda: e.tensor_tensor(degD[:, :], degD[:, :], ps[:, 7, 0:NB], ALU.add))
                p(lambda: e.transpose(ps[:, 4, 0:P], keys, ident[:, :]), tv.at())
                v(lambda: e.tensor_copy(keyT, ps[:, 4, 0:P]), tp.at())
                p(lambda: e.matmul(ps[:, 5, 0:KP], keyT, sel, start=True, stop=True), tv.at())
                v(lambda: e.scalar_tensor_tensor(out_rel[:, kb], bmin, -128.0, ps[:, 5, 0:KP], ALU.mult, ALU.add), tp.at())

        NP_SORT = 2 + 32 + T + 2
        NV_SRC = 6 + T + 3 + 32 + 6 + 8 + 7 + 64 + 5 + T + 2 + 2
        NV_DST = 10 + T + 3 + 32 + 6 + 8 + 7 + 64 + 5 + T + 14 + 2

        KT = SUP * KP
        ARR0 = 2 * NQ
        def gathers(e, layer, table, idx, with_edges):
            a0, st0 = ARR0 + layer * TILES, layer * KT
            if layer:
                e.wait_ge(s_ix, IX0[layer])
            e.tensor_copy(ixb[:, 0:NQ], idx[:, 0:NQ]).then_inc(s_ix, 1)
            if with_edges:
                e.tensor_copy(ixe[:, 0:NQ], perm[:, 0:NQ]).then_inc(s_ix, 1)
            ni = 2 if with_edges else 1

            def supertile(s, s_prev):
                for n in range(T // NQ):
                    e.wait_ge(s_arr, s * T + (a0 + NQ * n - NQ))
                    if s_prev is not None:
                        e.wait_ge(s_st, s_prev * KP + (st0 + (NQ * (n + 1) + NB - 1 if n < T // NQ - 1 else KP)))
                    c = ((n + 1) * NQ) % T
                    nxt = bass.ds(s * T + (n + 1) * NQ, NQ)
                    e.sem_inc(s_dum, 1)
                    e.tensor_copy(ixb[:, c:c + NQ], idx[:, nxt]).then_inc(s_ix, 1)
                    if with_edges:
                        e.tensor_copy(ixe[:, c:c + NQ], perm[:, nxt]).then_inc(s_ix, 1)
                    e.wait_ge(s_ix, s * (ni * (T // NQ)) + (IX0[layer] + ni * (n + 1)))
                    e.sem_inc(s_dum, 1)
                    for j in range(NQ):
                        t = n * NQ + j
                        e.indirect_dma_start(M[:, t, 0:P], None, table[:, :], bass.IndirectOffsetOnAxis(ap=ixb[:, t:t + 1], axis=0))\
                            .then_inc(s_g[t % 16], 16)
                    for j in range(NQ if with_edges else 0):
                        t = n * NQ + j
                        if j % 4 == 0:
                            e.wait_ge(s_tr, s * (T // 4) + (2 * n + 1 + j // 4))
                            e.sem_inc(s_dum, 1)
                        e.indirect_dma_start(er[:, j, :], None, edge_in[:, :],
                                             bass.IndirectOffsetOnAxis(ap=ixe[:, t:t + 1], axis=0)).then_inc(s_e[t % 16], 16)

            supertile(0, None)
            if SUP > 1:
                with e.Fori(0, SUP - 1) as it:
                    supertile(it + 1, it)

        IX0 = [0] * 4
        for l in range(1, 4):
            IX0[l] = IX0[l - 1] + TILES // NQ + 1

        def arrivals(e, layer, with_edges):
            with e.Fori(0, TILES // 16) as it:
                for j in range(16):
                    e.wait_ge(s_g[j], it * 16 + 16 * (layer * (TILES // 16) + 1))
                    if with_edges:
                        e.sem_inc(s_dum_s, 1)
                        e.wait_ge(s_e[j], it * 16 + 16)
                    e.sem_inc(s_arr, 1)

        N1 = T // SG
        PB = KI - N1
        PA = T // 8 - PB
        assert 0 <= PA <= N1

        def schedule(e, group, pair=None):
            if not pair:
                with e.Fori(0, SUP) as s:
                    with e.Fori(0, N1) as m:
                        group(s, m, m * SG + SG)
                    with e.Fori(0, KI - N1) as m:
                        group(s, m + N1, T)
                return
            with e.Fori(0, PB) as i:
                pair(i, i, None)

            def supertile(s, last):
                with e.Fori(0, PA) as i:
                    pair(s * (T // 8) + (i + PB), i + PB, lambda: group(s, i, i * SG + SG))
                with e.Fori(0, N1 - PA) as i:
                    group(s, i + PA, i * SG + (PA * SG + SG))
                with e.Fori(0, PB) as i:
                    if last:
                        group(s, i + N1, T)
                    else:
                        pair(s * (T // 8) + (i + T // 8), i, lambda: group(s, i + N1, T))

            with e.Fori(0, SUP - 1) as s:
                supertile(s, False)
            with e.Fori(SUP - 1, SUP) as s:
                supertile(s, True)

        def steps_pe(e, layer, row, regs, ready, r0, width, pair=None):
            def group(s, m, need):
                k0 = s * KP + m * SG
                e.load(regs, tab[row:row + 1, bass.ds(k0, SG)])
                tau_v = [e.snap(r, min_val=0, max_val=T - 1) for r in regs]
                e.wait_ge(ready, s * T + need + r0)
                for q in range(SG // 3):
                    e.wait_ge(s_oh, k0 + (layer * (KT + SG) + 3 * q + 3))
                    for i in range(3):
                        j = 3 * q + i
                        e.matmul(ps[:, q, i * W1C:i * W1C + width], oh[:, j, :],
                                 M[:, bass.ds(tau_v[j], 1), 0:width].rearrange("p a f -> p (a f)"),
                                 start=True, stop=True).then_inc(s_st, 1)

            schedule(e, group, pair)

        def steps_dve(e, layer, rel, row, regs, width, pair=None):
            def onehot(j, k):
                e.tensor_scalar(oh[:, j, :], iota128[:, :], rel[:, k], None, ALU.is_equal).then_inc(s_oh, 1)

            for j in range(SG):
                onehot(j, slice(j, j + 1))

            def group(s, m, need):
                k0 = s * KP + m * SG
                e.load(regs, tab[row + 32:row + 33, bass.ds(k0, SG)])
                b = [e.snap(r, min_val=0, max_val=NB - 1) for r in regs]
                for q in range(SG // 3):
                    e.wait_ge(s_st, k0 + (layer * KT + 3 * q + 3))
                    for i in range(3):
                        j = 3 * q + i
                        e.wait_ge(s_add, k0 + (layer * KT + j + 1))
                        a = acc[:, bass.ds(b[j], 1), 0:width].rearrange("p a f -> p (a f)")
                        e.tensor_tensor(a, a, ps[:, q, i * W1C:i * W1C + width], ALU.add).then_inc(s_add, 1)
                        onehot(j, bass.ds(k0 + (SG + j), 1))

            schedule(e, group, pair)

        def rows(ap, g, k=NG):
            return ap[0:ap.shape[0] // P * P, :].rearrange("(i p) f -> i p f", p=P)[bass.ds(g * NG, k), :, :].rearrange("i p f -> p i f")

        n3 = lambda ap: ap.rearrange("p (i f) -> p i f", f=P)
        SRC_X, DST_X = [x_in, x1, x2, x3], [x1, x2, x3, None]

        def node(e, role, layer, tl, tsx, tv, tp, ta):
            V, Q, A, S = role == "v", role == "p", role == "a", role == "s"

            def op(mine, sm, tally, make, marks, chain, gate=False):
                if mine:
                    for m in marks:
                        wait(e, m)
                    if chain:
                        wait(e, tally.at())
                    if gate:
                        e.sem_inc(s_dum_v, 1)
                    make().then_inc(sm, 1)
                tally.inc()

            v = lambda make, *marks, gate=False: op(V, s_nv, tv, make, marks, True, gate)
            p = lambda make, *marks: op(Q, s_np, tp, make, marks, False)
            a = lambda make, *marks: op(A, s_na, ta, make, marks, True)
            pf = lambda b, nb_: ps[:, b:b + nb_, :]
            banks = -(-NG // GA)

            def parts(k=NG):
                return [(b, b * GA, min(GA, NG - b * GA)) for b in range(banks)]

            def psn(b0):
                return [(ps[:, b0 + b, 0:n * P], i0 * P, n * P) for b, i0, n in parts()]

            def transpose_to(b0, src_, dst_, mark):
                def tr():
                    for i in range(NG):
                        o = ps[:, b0 + i // GA, (i % GA) * P:(i % GA) * P + P]
                        ins = e.transpose(o, src_[:, i * P:(i + 1) * P], ident[:, :])
                    return ins
                p(tr, mark)
                done = tp.at()

                def cp():
                    for o, c0, n in psn(b0):
                        ins = e.activation(dst_[:, c0:c0 + n], o, ACT.Copy)
                    return ins
                a(cp, done)

            xs, xd = SRC_X[layer], DST_X[layer]

            def body(g, last):
                full = NG - 1 if last else NG
                if S:
                    wait(e, tv.at())
                    e.sem_inc(s_dum_s, 1)
                    if last and layer == 0:
                        if full:
                            e.dma_start(n3(nxg)[:, 0:full, :], rows(xs, g, full)).then_inc(s_nl, 16)
                        else:
                            e.dma_start(n3(nxg)[0:LASTN, NG - 1, :], xs[(NB - 1) * P:N, :]).then_inc(s_nl, 16)
                        e.dma_start(n3(nxg)[0:LASTN, NG - 1, :], xs[(NB - 1) * P:N, :]).then_inc(s_nl, 16)
                    else:
                        e.dma_start(n3(nxg), rows(xs, g)).then_inc(s_nl, 16)
                tl.inc(32 if last and layer == 0 else 16)
                loaded = tl.at()
                ab = acc[:, bass.ds(g * NG, NG), :] if V else None
                if layer == 0:
                    dg = nst[:, 0:NG]
                    v(lambda: e.tensor_scalar(dg, ab[:, :, P:P + 1].rearrange("p a b -> p (a b)"), 1.0, None, ALU.max), loaded)
                    v(lambda: e.reciprocal(dg, dg))

                    def mean():
                        for i in range(NG):
                            ins = e.tensor_scalar(nag[:, i * P:(i + 1) * P], ab[:, i:i + 1, 0:P].rearrange("p a b -> p (a b)"), dg[:, i:i + 1], None, ALU.mult)
                        return ins
                    v(mean)
                    up = tv.at()
                    transpose_to(0, nxg, nxT, up)
                    transpose_to(2, nag, naT, up)
                    ready = ta.at()

                    def mm():
                        for i in range(NG):
                            o = ps[:, 4 + i // GA, (i % GA) * P:(i % GA) * P + P]
                            c = slice(i * P, (i + 1) * P)
                            e.matmul(o, nxT[:, c], wua_sb[:, :], start=True, stop=False)
                            ins = e.matmul(o, naT[:, c], wtu_sb[:, :], start=False, stop=True)
                        return ins
                    p(mm, ready)
                    done = tp.at()

                    def addb():
                        for o, c0, n in psn(4):
                            ins = e.tensor_tensor(n3(nh2[:, c0:c0 + n]), n3(o), bias[:, 0:1, :].to_broadcast([P, n // P, P]), ALU.add)
                        return ins
                    v(addb, done)
                    v(lambda: e.scalar_tensor_tensor(nz, nh2, 0.0, nxg, ALU.max, ALU.add))
                elif layer == 1:
                    dis = degD[:, bass.ds(g * NG, NG)] if V else None

                    def agg():
                        for i in range(NG):
                            ins = e.tensor_scalar(nag[:, i * P:(i + 1) * P], ab[:, i:i + 1, 0:P].rearrange("p a b -> p (a b)"), dis[:, i:i + 1], None, ALU.mult)
                        return ins
                    v(agg, loaded)
                    v(lambda: e.scalar_tensor_tensor(nag, nxg, eps_sb[:, 0:1], nag, ALU.mult, ALU.add))
                    v(lambda: e.tensor_tensor(nz, nag, nxg, ALU.add))
                elif layer in (2, 3):
                    v(lambda: e.scalar_tensor_tensor(n3(nag), n3(nxg), eps_sb[:, layer - 1:layer], ab[:, :, 0:P], ALU.mult, ALU.add), loaded)
                    transpose_to(0, nag, naT, tv.at())
                    nh = 1 if layer == 2 else HID // P
                    for h in range(nh):
                        wm = w21_sb[:, :] if layer == 2 else w31_sb[:, h * P:(h + 1) * P]
                        bc = b21c[:, 0:1] if layer == 2 else b31c[:, h:h + 1]
                        b0 = 2 + 2 * (h % 2)

                        def up_():
                            for o, c0, n in psn(b0):
                                ins = e.matmul(o, wm, naT[:, c0:c0 + n], start=True, stop=True)
                            return ins
                        p(up_, ta.at())

                        def relu():
                            for o, c0, n in psn(b0):
                                ins = e.activation(nhT[:, h * NW + c0:h * NW + c0 + n], o, ACT.Relu, bias=bc)
                            return ins
                        a(relu, tp.at())

                    def down():
                        for i in range(NG):
                            o = ps[:, 6 + i // GA, (i % GA) * P:(i % GA) * P + P]
                            for h in range(nh):
                                wm = w22_sb[:, :] if layer == 2 else w32_sb[:, h, :]
                                ins = e.matmul(o, nhT[:, h * NW + i * P:h * NW + (i + 1) * P], wm, start=h == 0, stop=h == nh - 1)
                        return ins
                    p(down, ta.at())
                    done = tp.at()
                    br = 1 if layer == 2 else 2

                    def addb():
                        for o, c0, n in psn(6):
                            ins = e.tensor_tensor(n3(nh2[:, c0:c0 + n]), n3(o), bias[:, br:br + 1, :].to_broadcast([P, n // P, P]), ALU.add)
                        return ins
                    v(addb, done)
                    v(lambda: e.tensor_tensor(nz, nh2, nxg, ALU.add))

                def stats():
                    for i in range(NG):
                        ins = e.bn_stats(nst[:, i * 6:(i + 1) * 6], nz[:, i * P:(i + 1) * P])
                    return ins
                v(stats)

                def aggr():
                    for i in range(NG):
                        ins = e.bn_aggr(nmv[:, 2 * i:2 * i + 2], nst[:, i * 6:(i + 1) * 6])
                    return ins
                v(aggr, gate=True)
                mv = nmv.rearrange("p (i c) -> p i c", c=2)
                a(lambda: e.activation(nrs[:, 0:NG], mv[:, :, 1:2].rearrange("p a b -> p (a b)"), ACT.Sqrt, bias=eps_sb[:, 3:4]), tv.at())
                v(lambda: e.reciprocal(nrs[:, NG:2 * NG], nrs[:, 0:NG]), ta.at())
                stored = tsx.at()

                def norm():
                    for i in range(NG):
                        ins = e.tensor_scalar(nout[:, i * P:(i + 1) * P], nz[:, i * P:(i + 1) * P], nmv[:, 2 * i:2 * i + 1],
                                              nrs[:, NG + i:NG + i + 1], ALU.subtract, ALU.mult)
                    return ins
                v(norm, stored)
                nd = 1
                if layer == 0:
                    dis = degD[:, bass.ds(g * NG, NG)] if V else None

                    def scale():
                        for i in range(NG):
                            ins = e.tensor_scalar(nag[:, i * P:(i + 1) * P], nout[:, i * P:(i + 1) * P], dis[:, i:i + 1], None, ALU.mult)
                        return ins
                    v(scale)
                    nd = 2
                elif layer == 2:
                    v(lambda: e.tensor_tensor(n3(nag), n3(nout), bias[:, 3:4, :].to_broadcast([P, NG, P]), ALU.add))
                    nd = 2
                if S:
                    wait(e, tv.at())
                    e.sem_inc(s_dum_s, 1)
                    if layer == 3 and last:
                        if full:
                            e.dma_start(rows(out, g, full), n3(nout)[:, 0:full, :]).then_inc(s_ns, 16)
                        else:
                            e.dma_start(out[(NB - 1) * P:N, :], n3(nout)[0:LASTN, NG - 1, :]).then_inc(s_ns, 16)
                        e.dma_start(out[(NB - 1) * P:N, :], n3(nout)[0:LASTN, NG - 1, :]).then_inc(s_ns, 16)
                    else:
                        e.dma_start(rows(out if layer == 3 else xd, g), n3(nout)).then_inc(s_ns, 16)
                        if nd == 2:
                            e.dma_start(rows(t1 if layer == 0 else t3, g), n3(nag)).then_inc(s_ns, 16)
                tsx.inc(32 if (layer == 3 and last) else 16 * nd)
                if nd == 2:
                    v(lambda: e.memset(nrs[:, 0:1], 0.0), tsx.at())

            if layer == 0:
                v(lambda: e.memset(nxg, 0.0), *([(s_st, KT, ())] if V else []))
            per = NODE_PER[layer]
            special = layer in (0, 3)
            trips = GROUPS - 1 if special else GROUPS
            if trips:
                with loop(e, trips, (tl, 16), (tsx, per[0]), (tv, per[1]), (tp, per[2]), (ta, per[3])) as g:
                    body(g, False)
            if special:
                body(GROUPS - 1, True)

        NODE_PER = [(32, 11, 3, 3), (16, 7, 0, 1), (32, 9, 3, 3), (16, 7, 6, 6)]

        U0 = 3 * TILES + ARR0
        MV0 = 8

        def edge_pe(e):
            def pair(pi, loc, then):
                for h in range(2):
                    e.wait_ge(s_arr, pi * 8 + (U0 + 4 * h + 4))
                    e.wait_ge(s_et, pi * 2 + (h + 1))
                    for j in range(4):
                        ins = e.transpose(ps[:, 4, j * P:(j + 1) * P], er[:, 4 * h + j, :], ident[:, :])
                    ins.then_inc(s_tr, 1)
                    e.wait_ge(s_et, pi * 2 + (h + 2))
                    e.wait_ge(s_vv, pi * 2 + (h + 1))
                    for j in range(4):
                        ins = e.matmul(ps[:, 5 + h, j * P:(j + 1) * P], et[:, h, j * P:(j + 1) * P], we_sb[:, :],
                                       start=True, stop=True)
                    ins.then_inc(s_u, 1)
                if then:
                    then()
            return pair

        def edge_act(e):
            def pair(pi, loc, then):
                for h in range(2):
                    e.wait_ge(s_tr, pi * 2 + (h + 3))
                    e.activation(et[:, h, :], ps[:, 4, :], ACT.Copy).then_inc(s_et, 1)
                for h in range(2):
                    e.wait_ge(s_vv, pi * 2 + (h + 3))
                    e.activation(eb[:, h, :], vb[:, h, :], ACT.Exp).then_inc(s_ex, 1)
            return pair

        def edge_dve(e):
            def pair(pi, loc, then):
                def m_at(h):
                    return M[:, bass.ds(loc * 8 + 4 * h, 4), 0:P]
                n4 = lambda ap: ap.rearrange("p (t f) -> p t f", f=P)
                for h in range(2):
                    e.wait_ge(s_mv, pi * 8 + (MV0 - 4 + 4 * h))
                    e.wait_ge(s_u, pi * 2 + (h + 1))
                    e.tensor_tensor(n4(vb[:, h, :]), m_at(h), n4(ps[:, 5 + h, :]), ALU.add).then_inc(s_vv, 1)
                if then:
                    then()
                chainops = [
                    lambda h: e.tensor_scalar(eb[:, h, :], eb[:, h, :], 1e9, None, ALU.min),
                    lambda h: e.scalar_tensor_tensor(wb[:, h, :], eb[:, h, :], 2.0, eb[:, h, :], ALU.add, ALU.mult),
                    lambda h: e.tensor_scalar(eb[:, h, :], wb[:, h, :], 2.0, None, ALU.add),
                    lambda h: e.reciprocal(eb[:, h, :], eb[:, h, :]),
                    lambda h: e.tensor_tensor(wb[:, h, :], wb[:, h, :], eb[:, h, :], ALU.mult),
                ]
                for i, make in enumerate(chainops):
                    for h in range(2):
                        if i == 0:
                            e.wait_ge(s_ex, pi * 2 + (h + 1))
                        else:
                            e.wait_ge(s_c, pi * 10 + (2 * (i - 1) + h + 1))
                        make(h).then_inc(s_c, 1)
                for h in range(2):
                    e.wait_ge(s_c, pi * 10 + (9 + h))
                    e.tensor_tensor(m_at(h), n4(wb[:, h, :]), n4(vb[:, h, :]), ALU.mult).then_inc(s_mv, 4)
            return pair

        F, rem = E // SE, E % SE
        r_full, r_tail = rem // T, rem % T

        def node_tallies():
            return [Tally(s) for s in (s_nl, s_ns, s_nv, s_np, s_na)]


        def bcast_row(ap, n):
            return ap.rearrange("(a n) -> a n", a=1).to_broadcast([P, n])

        def raw_views(dst, src):
            if F:
                yield dst[:, 0:F * T].rearrange("p (s c) -> p s c", c=T), src[0:F * SE].rearrange("(s p c) -> p s c", p=P, c=T)
            if r_full:
                yield dst[0:r_full, F * T:TILES], src[F * SE:F * SE + r_full * T].rearrange("(p c) -> p c", c=T)
            if r_tail:
                yield dst[r_full:r_full + 1, F * T:F * T + r_tail], src[F * SE + r_full * T:E].rearrange("(p c) -> p c", p=1)

        weight_loads = [
            (wt_sb, Wt), (wua_sb[:, :], Wu[0:P, :]), (wub_sb, Wu[P:2 * P, :]), (w21_sb[:, :], W21), (w22_sb[:, :], W22),
            (we_sb[:, :], We), (w31_sb[:, :], W31[0:P, :]), (w31g_sb, W31[P:2 * P, :]),
            (w32_sb[:, :, :], W32.rearrange("(h p) n -> p h n", p=P)),
            (bias[:, 0, :], bcast_row(bu, P)), (bias[:, 1, :], bcast_row(b22, P)), (bias[:, 2, :], bcast_row(b32, P)),
            (bias[:, 3, :], bcast_row(be, P)),
            (eps_sb[:, 0:1], bcast_row(eps1, 1)), (eps_sb[:, 1:2], bcast_row(eps2, 1)),
            (eps_sb[:, 2:3], eps3.to_broadcast([P, 1])),
            (b21c[:, :], b21.rearrange("(p a) -> p a", a=1)), (globc[:, :], glob.rearrange("a p -> p a")),
            (b31c[:, :], b31.rearrange("(h p) -> p h", p=P)),
        ]
        raw_loads = [v for d, s_ in ((raw_s, src_in), (raw_d, dst_in), (raw_w, w_in.rearrange("e a -> (e a)"))) for v in raw_views(d, s_)]
        NLD = 16 * (len(weight_loads) + len(raw_loads))
        NCST, TABLES = 21, [x_in, t1, x2, t3]
        SQ_AT = 6 + SUP * (NV_SRC + NV_DST) + 3
        NS_DONE = [32 * GROUPS, 48 * GROUPS, 80 * GROUPS]

        block = ctx.enter_context(nc.Block())

        @block.sync
        def _(e):
            e.wait_ge(s_cst, 3)
            n_node = node_tallies()
            for d, s_ in weight_loads + raw_loads:
                e.dma_start(d, s_).then_inc(s_ld, 16)
            for layer in range(4):
                arrivals(e, layer, layer == 3)
                e.wait_ge(s_st, (layer + 1) * KT)
                node(e, "s", layer, *n_node)
            e.wait_ge(s_ns, n_node[1].n)

        @block.gpsimd
        def _(e):
            for s_, k in ((s_arr, ARR0), (s_tr, 2), (s_et, 1), (s_vv, 2), (s_add, 1)):
                e.sem_inc(s_, k)
            e.memset(raw_s[:, F * T:TILES] if rem else raw_s[:, 0:1], NB * P - 1).then_inc(s_cst, 1)
            e.memset(raw_d[:, F * T:TILES] if rem else raw_d[:, 0:1], NB * P - 1).then_inc(s_cst, 1)
            e.memset(raw_w[:, F * T:TILES] if rem else raw_w[:, 0:1], 0.0).then_inc(s_cst, 1)
            c = [3]

            def k(ins):
                ins.then_inc(s_cst, 1)
                c[0] += 1

            k(e.memset(ident[:, :], 0.0))
            k(e.memset(ones_f[:, :], 1.0))
            k(e.memset(ones_b[:, :], 1.0))
            k(e.memset(ltri[:, :], 1.0))
            k(e.memset(bigcol[:, :], 0.0))
            k(e.memset(degD[:, :], 0.0))
            k(e.memset(gS[:, TILES:TILES + NQ], 0))
            k(e.memset(gD[:, TILES:TILES + NQ], 0))
            k(e.memset(perm[:, TILES:TILES + NQ], 0))
            k(e.memset(eps_sb[:, 3:4], LN_EPS))
            k(e.memset(relS[:, SUP * KP:SUP * KP + SG], -1.0))
            k(e.memset(relD[:, SUP * KP:SUP * KP + SG], -1.0))
            it_ = dict(allow_small_or_imprecise_dtypes=True)
            k(e.iota(iota128[:, :], [[1, P]], base=0, channel_multiplier=0, **it_))
            k(e.iota(iotaK[:, :], [[1, KP]], base=0, channel_multiplier=0, **it_))
            k(e.iota(iota_p[:, :], [[0, 1]], base=0, channel_multiplier=1, **it_))
            k(e.iota(neg128p[:, :], [[0, 1]], base=0, channel_multiplier=-P, **it_))
            k(e.iota(sbase[:, :], [[SE, SUP]], base=0, channel_multiplier=0, **it_))
            e.wait_ge(s_cst, c[0])
            k(e.affine_select(out=ident[:, :], in_=ident[:, :], compare_op=ALU.not_equal, fill=1.0, base=0,
                              pattern=[[-1, P]], channel_multiplier=1))
            k(e.affine_select(out=ltri[:, :], in_=ltri[:, :], compare_op=ALU.is_ge, fill=0.0, base=-1,
                              pattern=[[1, P]], channel_multiplier=-1))
            k(e.affine_select(out=bigcol[:, :], in_=bigcol[:, :], compare_op=ALU.is_ge, fill=1e6, base=NB - 1,
                              pattern=[[0, 1]], channel_multiplier=-1))
            assert c[0] == NCST + 2, c[0]
            for layer in range(4):
                e.wait_ge(s_mv, layer + 1)
                gathers(e, layer, TABLES[layer], gS if layer < 2 else gD, layer == 3)

        @block.vector
        def _(e):
            tv, tp = Tally(s_v), Tally(s_p)
            e.wait_ge(s_cst, NCST + 2)
            e.wait_ge(s_ld, NLD)

            def v(make, *marks):
                for m in marks:
                    wait(e, m)
                if tv.n:
                    wait(e, tv.at())
                make().then_inc(s_v, 1)
                tv.inc()

            v(lambda: e.tensor_copy(iotaNb[:, :], iota128[:, 0:NB]))
            v(lambda: e.tensor_copy(iota128b[:, :], iota128[:, :]))
            v(lambda: e.tensor_scalar(eps_sb[:, 0:3], eps_sb[:, 0:3], 1.0, None, ALU.add))
            tp.inc()
            v(lambda: e.tensor_copy(keys, ps[:, 0, 0:P]), tp.at())
            tp.inc()
            v(lambda: e.tensor_copy(wtu_sb[:, :], ps[:, 1, 0:P]), tp.at())
            v(lambda: e.tensor_tensor(b31c[:, :], b31c[:, :], ps[:, 1, P:P + HID // P], ALU.add))
            sort(e, "v", tv, tp, raw_s, raw_d, None, relS, gS, 0)
            sort(e, "v", tv, tp, raw_d, raw_s, raw_w, relD, gD, 64)
            v(lambda: e.tensor_scalar(degm[:, :], degD[:, :], 0.5, None, ALU.is_gt))
            v(lambda: e.tensor_scalar(degD[:, :], degD[:, :], 1.0, None, ALU.max))
            v(lambda: e.reciprocal(degD[:, :], degD[:, :]))
            assert tv.n == SQ_AT, tv.n
            e.wait_ge(s_a, 1)
            v(lambda: e.tensor_tensor(degD[:, :], degD[:, :], degm[:, :], ALU.mult))
            regs = [e.alloc_register(f"node_tile{j}") for j in range(SG)]
            n_node = node_tallies()
            for layer in range(4):
                v(lambda: e.memset(acc_flat, 0.0))
                if layer == 0:
                    v(lambda: e.memset(M[:, :, P:W1C], 1.0))
                e.wait_ge(s_v, tv.n)
                if layer:
                    e.wait_ge(s_ns, NS_DONE[layer - 1])
                e.sem_inc(s_mv, 1 if layer < 3 else MV0 - 3)
                steps_dve(e, layer, relS if layer < 2 else relD, 0 if layer < 2 else 64, regs, W1C if layer == 0 else P,
                          edge_dve(e) if layer == 3 else None)
                e.wait_ge(s_add, (layer + 1) * KT + 1)
                node(e, "v", layer, *n_node)
                e.wait_ge(s_nv, n_node[2].n)

        @block.tensor
        def _(e):
            tv, tp = Tally(s_v), Tally(s_p)
            e.wait_ge(s_cst, NCST + 2)
            e.wait_ge(s_ld, NLD)
            e.transpose(ps[:, 0, 0:P], wt_sb, ident[:, :]).then_inc(s_p, 1)
            tv.inc(4)
            wait(e, tv.at())
            e.matmul(ps[:, 1, 0:P], keys, wub_sb, start=True, stop=True)
            for h in range(HID // P):
                ins = e.matmul(ps[:, 1, P + h:P + h + 1], w31g_sb[:, h * P:(h + 1) * P], globc[:, :], start=True, stop=True)
            ins.then_inc(s_p, 1)
            tp.inc(2)
            tv.inc(2)
            sort(e, "p", tv, tp, raw_s, raw_d, None, relS, gS, 0)
            sort(e, "p", tv, tp, raw_d, raw_s, raw_w, relD, gD, 64)
            regs = [e.alloc_register(f"edge_tile{j}") for j in range(SG)]
            n_node = node_tallies()
            for layer in range(4):
                ready, r0 = ((s_arr, ARR0), (s_arr, ARR0 + TILES), (s_m, 0), (s_mv, MV0))[layer]
                steps_pe(e, layer, 0 if layer < 2 else 64, regs, ready, r0, W1C if layer == 0 else P,
                         edge_pe(e) if layer == 3 else None)
                node(e, "p", layer, *n_node)

        @block.scalar
        def _(e):
            e.wait_ge(s_v, SQ_AT)
            n_node = node_tallies()
            e.activation(degD[:, :], degD[:, :], ACT.Sqrt).then_inc(s_a, 1)
            for layer in range(4):
                if layer == 2:
                    with e.Fori(0, SUP) as s:
                        with e.Fori(0, T) as t:
                            e.wait_ge(s_arr, s * T + t + (ARR0 + 2 * TILES + 1))
                            e.sem_inc(s_dum_a, 1)
                            m = M[:, bass.ds(t, 1), 0:P].rearrange("p a f -> p (a f)")
                            e.activation(m, m, ACT.Copy, scale=wD[:, bass.ds(s * T + t, 1)]).then_inc(s_m, 1)
                if layer == 3:
                    schedule(e, lambda s, m, need: None, edge_act(e))
                node(e, "a", layer, *n_node)


_INS = ["x", "src", "dst", "edge_attr_128", "edge_weight1", "L0_gnn_W_t", "L0_gnn_W_u", "L0_gnn_b_u", "L1_gnn_eps",
        "L2_gnn_eps", "L2_gnn_W1", "L2_gnn_b1", "L2_gnn_W2", "L2_gnn_b2", "L3_gnn_globals_g", "L3_gnn_W_e_k",
        "L3_gnn_W_e_b", "L3_gnn_eps", "L3_gnn_W1", "L3_gnn_b1", "L3_gnn_W2", "L3_gnn_b2"]


def kernel(**inputs):
    import numpy as _np
    import concourse.bacc as _bacc
    from concourse import mybir as _mybir
    from concourse.bass_utils import run_bass_kernel_spmd as _run

    nc = _bacc.Bacc("TRN2", target_bir_lowering=False, num_devices=1)
    arrays, args = {}, []
    for name in _INS:
        a = _np.ascontiguousarray(inputs[name])
        arrays[f"in_{name}"] = a
        args.append(nc.dram_tensor(f"in_{name}", a.shape, _mybir.dt.from_np(a.dtype), kind="ExternalInput").ap())
    args.append(nc.dram_tensor("out_x", inputs["x"].shape, _mybir.dt.float32, kind="ExternalOutput").ap())
    graph_layers(nc, *args)
    return _run(nc, [arrays], core_ids=[0]).results[0]["out_x"]
```

```python
import concourse.bass as bass
from concourse import mybir
from contextlib import ExitStack, contextmanager

P = 128
T = 128
SE = P * T
W1C = P + 1
SG = 12
NQ = 8
HID = 512
LN_EPS = 1e-5


class Tally:

    def __init__(self, sem):
        self.sem, self.n, self.terms = sem, 0, ()

    def inc(self, k=1):
        self.n += k

    def at(self):
        return self.sem, self.n, self.terms


def wait(e, mark):
    sem, n, terms = mark
    v = n
    for var, per in terms:
        v = var * per + v
    e.wait_ge(sem, v)


@contextmanager
def loop(e, trips, *tallies_per):
    with e.Fori(0, trips) as it:
        start = [(t, t.n, t.terms) for t, _ in tallies_per]
        for t, per in tallies_per:
            t.terms = t.terms + ((it, per),)
        yield it
        for (t, n0, terms), (_, per) in zip(start, tallies_per):
            assert t.n - n0 == per, (t.sem, t.n - n0, per)
            t.n, t.terms = n0 + per * trips, terms


@contextmanager
def count(trips, *tallies_per):
    start = [(t, t.n) for t, _ in tallies_per]
    yield 0
    for (t, n0), (_, per) in zip(start, tallies_per):
        assert t.n - n0 == per, (t.sem, t.n - n0, per)
        t.n = n0 + per * trips


def graph_layers(nc, x_in, src_in, dst_in, edge_in, w_in, Wt, Wu, bu, eps1, eps2, W21, b21, W22, b22,
                 glob, We, be, eps3, W31, b31, W32, b32, out):
    f32, bf16, i32 = mybir.dt.float32, mybir.dt.bfloat16, mybir.dt.int32
    ALU, ACT, AX = mybir.AluOpType, mybir.ActivationFunctionType, mybir.AxisListType
    N, E = x_in.shape[0], src_in.shape[0]
    NB = -(-N // P)
    SUP = -(-E // SE)
    TILES = SUP * T
    K = T + NB - 1
    KI = -(-K // SG)
    KP = KI * SG
    NG = next(g for g in (7, 4, 2, 1) if NB % g == 0)
    GROUPS = NB // NG
    LASTN = N - (NB - 1) * P
    GA = min(4, NG)
    x1, x2, x3 = (nc.dram_tensor(n, (NB * P, P), f32, kind="Internal").ap() for n in ("x1", "x2", "x3"))
    t1, t3 = (nc.dram_tensor(n, (NB * P, P), f32, kind="Internal").ap() for n in ("t1", "t3"))

    with ExitStack() as ctx:
        ctx.enter_context(nc.allow_non_contiguous_dma("index blocks and biases"))

        def sb(name, shape, dt=f32):
            return ctx.enter_context(nc.sbuf_tensor(name, shape, dt))

        def sem(name):
            return ctx.enter_context(nc.semaphore(name))

        M = sb("M", [P, T, W1C])
        acc = sb("acc", [P, NB, W1C])
        acc_flat = acc[:, :, :].rearrange("p a f -> p (a f)")
        M_flat = M[:, :, :].rearrange("p a f -> p (a f)")
        relS, relD = sb("relS", [P, max(SUP * KP + SG, 16 * P)]), sb("relD", [P, max(SUP * KP + SG, TILES)])
        tab = sb("tab", [P, SUP * KP], i32)
        gS, gD = sb("gS", [P, TILES + T // 2], i32), sb("gD", [P, TILES + T // 2], i32)
        perm = sb("perm", [P, TILES + T // 2], i32)
        wD = sb("wD", [P, TILES])
        ixb, ixe = sb("ixb", [P, T], i32), sb("ixe", [P, T], i32)
        oh = sb("oh", [P, SG, P])
        relc = sb("relc", [P, SG])
        ident, ones_f, iota128 = sb("ident", [P, P]), sb("ones_f", [P, P]), sb("iota128", [P, P])
        iotaK, iota_p, neg128p, bigcol = sb("iotaK", [P, KP]), sb("iota_p", [P, 1]), sb("neg128p", [P, 1]), sb("bigcol", [P, 1])
        sbase = sb("sbase", [P, SUP])
        ones_b, ltri, iotaNb = sb("ones_b", [P, P], bf16), sb("ltri", [P, P], bf16), sb("iotaNb", [P, NB], bf16)
        iota128b = sb("iota128b", [P, P], bf16)
        degD = sb("degD", [P, NB])
        eps_sb = sb("eps_sb", [P, 4])
        wtu_sb, wua_sb = sb("wtu_sb", [P, P]), sb("wua_sb", [P, P])
        w21_sb, w22_sb, we_sb = (sb(n, [P, P]) for n in ("w21_sb", "w22_sb", "we_sb"))
        w31_sb, w32_sb = sb("w31_sb", [P, HID]), sb("w32_sb", [P, HID // P, P])
        bias = sb("bias", [P, 4, P])
        b21c, globc, b31c = sb("b21c", [P, 1]), sb("globc", [P, 1]), sb("b31c", [P, HID // P])
        degm = sb("degm", [P, NB])
        unsorted = sb("unsorted", [P, 1], i32)

        arena = [M_flat, 0, T * W1C]

        def take(cols, dt=f32):
            n = cols if dt != bf16 else -(-cols // 2)
            v = arena[0][:, arena[1]:arena[1] + n]
            arena[1] += n
            assert arena[1] <= arena[2]
            return v if dt == f32 else v.bitcast(dt)

        raw_s, raw_d, raw_w = take(TILES, i32), take(TILES, i32), take(TILES)
        gsum, cx = (take(g * NB, bf16).rearrange("p (g b) -> p g b", b=NB) for g in (32, 34))
        t2 = take(32 * 2 * NB, bf16).rearrange("p (g b) -> p g b", b=2 * NB)
        ohl = take(8 * P).rearrange("p (j c) -> p j c", c=P)
        oht = take(8 * 3 * P).rearrange("p (j c) -> p j c", c=3 * P)
        arena[:] = [acc_flat, 0, NB * W1C]
        ohh_flat = take(T * NB // 2)
        ohh = ohh_flat.bitcast(bf16).rearrange("p (t b) -> p t b", b=NB)
        ti = [take(T, i32) for _ in range(3)]
        khi, kf, gf, pos = (take(T) for _ in range(4))
        packed = take(6 * T).rearrange("p (a t) -> p a t", t=T)
        lane, tile_f, klo = (packed[:, i, :] for i in range(3))
        pays = [packed[:, 3 + i, :] for i in range(3)]
        col8 = take(2 * 6 * 8).rearrange("p (r a t) -> p r a t", r=2, a=6)
        tot, endp, base_, endt = (take(NB) for _ in range(4))
        cum0, cmp = take(NB, bf16), take(KP, bf16)
        endi, lcol = take(NB, i32), take(2)
        bmin, tau, sel = take(KP), take(KP), take(KP)
        prod = take(8 * NB).rearrange("p (g b) -> p g b", b=NB)
        ohlo = take(8 * P, bf16).rearrange("p (j c) -> p j c", c=P)
        keys, keyT = take(P), take(P)
        er, et = sb("er", [P, NQ, P]), sb("et", [P, 2, 4 * P])
        relS_flat = relS[:, :]
        vb, eb = (relS_flat[:, i * 8 * P:(i + 1) * 8 * P].rearrange("p (g c) -> p g c", g=2) for i in range(2))
        eb2 = relS_flat[:, 8 * P:16 * P]
        next_d = relD[:, 0:TILES].bitcast(i32)
        arena[:] = [M_flat, 0, T * W1C]
        NW = NG * P
        nxg, nag, nxT, naT, nh2, nz, nout = (take(NW) for _ in range(7))
        nhT = take(NW * (HID // P))
        nst, nmv, nrs = take(NG * 6), take(NG * 2), take(NG * 2)
        oh_flat = oh[:, :, :].rearrange("p a f -> p (a f)")
        wt_sb, wub_sb, w31g_sb = oh_flat[:, 0:P], oh_flat[:, P:2 * P], oh_flat[:, 2 * P:2 * P + HID]

        ps = ctx.enter_context(nc.psum_tensor("ps", [P, 8, 512], f32))

        s_ld, s_cst, s_v, s_p, s_a = (sem(n) for n in ("s_ld", "s_cst", "s_v", "s_p", "s_a"))
        s_g = [sem(f"s_g{i}") for i in range(16)]
        s_e = [sem(f"s_e{i}") for i in range(16)]
        s_arr, s_oh, s_st, s_add, s_ix, s_m = (sem(n) for n in ("s_arr", "s_oh", "s_st", "s_add", "s_ix", "s_m"))
        s_rc, s_fv, s_fp, s_etail, s_tr, s_et, s_u, s_vv, s_ex, s_mv, s_c = (
            sem(n) for n in ("s_rc", "s_fv", "s_fp", "s_etail", "s_tr", "s_et", "s_u", "s_vv", "s_ex", "s_mv", "s_c"))
        s_dum, s_dum_v, s_dum_a, s_dum_s = (sem(n) for n in ("s_dum", "s_dum_v", "s_dum_a", "s_dum_s"))
        s_nl, s_ns, s_nv, s_np, s_na = (sem(n) for n in ("s_nl", "s_ns", "s_nv", "s_np", "s_na"))

        def step_table(e, v, p, tv, tp, row, kb):
            v(lambda: e.tensor_copy(endi, endp))
            v(lambda: e.tensor_scalar(endi, endi, 7, None, ALU.logical_shift_right))
            v(lambda: e.tensor_scalar(endt, endi, T - 1, None, ALU.min))
            v(lambda: e.tensor_tensor(endt, endt, iota128[:, 0:NB], ALU.add))
            v(lambda: e.tensor_tensor(endt, endt, ident[:, 0:NB], ALU.mult))
            v(lambda: e.tensor_reduce(lcol[:, 0:1], endt, AX.X, ALU.add))
            v(lambda: e.tensor_tensor(lcol[:, 1:2], lcol[:, 0:1], bigcol[:, :], ALU.add))
            v(lambda: e.tensor_scalar(cmp, iotaK[:, :], lcol[:, 1:2], None, ALU.is_gt))
            p(lambda: e.matmul(ps[:, 7, 128:128 + KP], ones_b[:, :], cmp, start=True, stop=True), tv.at())
            v(lambda: e.tensor_scalar(bmin, ps[:, 7, 128:128 + KP], float(NB - 1), None, ALU.min), tp.at())
            v(lambda: e.tensor_tensor(tau, iotaK[:, :], bmin, ALU.subtract))
            v(lambda: e.tensor_scalar(tau, tau, float(T - 1), None, ALU.min))
            v(lambda: e.tensor_scalar(sel, tau, iota_p[:, 0:1], None, ALU.is_equal))
            v(lambda: e.memset(sel[:, K:KP], 0.0))
            v(lambda: e.tensor_copy(tab[row:row + 1, kb], tau[row:row + 1, :]), gate=True)
            v(lambda: e.tensor_copy(tab[row + 32:row + 33, kb], bmin[row + 32:row + 33, :]), gate=True)

        def sort(e, role, tv, tp, key, gat, wts, out_rel, out_g, row):
            V, Q = role == "v", role == "p"
            lp = (lambda trips, *t: loop(e, trips, *t)) if role in "vp" else (lambda trips, *t: count(trips, *t))

            def v(make, *marks, chain=True, gate=False):
                if V:
                    for m in marks:
                        wait(e, m)
                    if chain:
                        wait(e, tv.at())
                    if gate:
                        e.sem_inc(s_dum_v, 1)
                    make().then_inc(s_v, 1)
                tv.inc()

            def p(make, *marks):
                if Q:
                    for m in marks:
                        wait(e, m)
                    make().then_inc(s_p, 1)
                tp.inc()

            npay = 3 if wts is not None else 2
            per_v = (NV_DST if wts is not None else NV_SRC)
            per_p = NP_SORT
            with lp(SUP, (tv, per_v), (tp, per_p)) as s:
                blk = bass.ds(s * T, T) if (V or Q) else slice(0, T)
                v(lambda: e.tensor_scalar(ti[0], key[:, blk], 7, None, ALU.logical_shift_right))
                v(lambda: e.tensor_copy(khi, ti[0]))
                v(lambda: e.tensor_copy(kf, key[:, blk]), gate=True)
                v(lambda: e.tensor_copy(gf, gat[:, blk]), gate=True)
                if wts is None:
                    v(lambda: e.tensor_copy(pays[0], kf))
                    v(lambda: e.tensor_scalar(pays[1], gf, float(N - 1), None, ALU.min))
                else:
                    v(lambda: e.tensor_scalar(gf, gf, float(N - 1), 128.0, ALU.min, ALU.mult))
                    v(lambda: e.tensor_scalar(pays[0], gf, iota_p[:, 0:1], None, ALU.add))
                    v(lambda: e.scalar_tensor_tensor(pays[1], kf, 128.0, iota128[:, :], ALU.mult, ALU.add))
                    v(lambda: e.tensor_copy(pays[2], wts[:, blk]), gate=True)
                    v(lambda: e.tensor_scalar(ti[1], key[:, blk], 127, None, ALU.bitwise_and))
                    v(lambda: e.tensor_copy(klo, ti[1]))
                split = tv.at()
                with lp(T // 8, (tv, 1)) as c:
                    v(lambda: e.tensor_tensor(ohh[:, bass.ds(c * 8, 8), :],
                                              iotaNb[:, :].rearrange("p (a b) -> p a b", a=1).to_broadcast([P, 8, NB]),
                                              khi[:, bass.ds(c * 8, 8)].rearrange("p (a b) -> p a b", b=1).to_broadcast([P, 8, NB]),
                                              ALU.is_equal), split, chain=False)
                oh4 = ohh.rearrange("p (g c) b -> p g (c b)", c=4)
                v(lambda: e.tensor_tensor(t2, oh4[:, :, 0:2 * NB], oh4[:, :, 2 * NB:4 * NB], ALU.add))
                v(lambda: e.tensor_tensor(gsum, t2[:, :, 0:NB], t2[:, :, NB:2 * NB], ALU.add))
                v(lambda: e.memset(cx[:, 0, :], 0.0))
                for g in range(32):
                    v(lambda: e.tensor_tensor(cx[:, g + 1, :], cx[:, g, :], gsum[:, g, :], ALU.add))
                p(lambda: e.matmul(ps[:, 7, 0:NB], ones_b[:, :], cx[:, 32, :], start=True, stop=True), tv.at())
                v(lambda: e.tensor_copy(tot, ps[:, 7, 0:NB]), tp.at())
                v(lambda: e.tensor_tensor_scan(endp, ones_f[:, 0:NB], tot, 0.0, ALU.mult, ALU.add))
                v(lambda: e.tensor_tensor(base_, endp, tot, ALU.subtract))
                v(lambda: e.tensor_scalar(base_, base_, neg128p[:, 0:1], 0.0, ALU.add, ALU.max))
                v(lambda: e.tensor_scalar(cum0, base_, 128.0, None, ALU.min))
                v(lambda: e.tensor_tensor(cx[:, 0:32, :], cx[:, 0:32, :],
                                          cum0.rearrange("p (a b) -> p a b", a=1).to_broadcast([P, 32, NB]), ALU.add))
                biased = tv.at()
                kb = bass.ds(s * KP, KP) if V else slice(0, KP)
                step_table(e, v, p, tv, tp, row, kb)
                v0 = tv.at()
                with lp(16, (tv, 4), (tp, 2)) as h:
                    ranks = []
                    for i in range(2):
                        g = h * 2 + i if (V or Q) else 0
                        o = ps[:, 4 + i, 0:4 * NB].rearrange("p (c b) -> p c b", b=NB)

                        def rank():
                            e.matmul(o, ltri[:, :], ohh[:, bass.ds(g * 4, 4), :], start=True, stop=False)
                            e.matmul(o, ones_b[:, :], cx[:, bass.ds(g, 1), :].to_broadcast([P, 4, NB]), start=False, stop=False)
                            for c in range(3):
                                i_ = e.matmul(o[:, c + 1:4, :], ones_b[:, :],
                                              ohh[:, bass.ds(g * 4 + c, 1), :].to_broadcast([P, 3 - c, NB]),
                                              start=False, stop=c == 2)
                            return i_

                        p(rank, (s_v, tv.n - (2 - 2 * i), tv.terms))
                        ranks.append(tp.at())
                    for i in range(2):
                        g = h * 2 + i if (V or Q) else 0
                        o = ps[:, 4 + i, 0:4 * NB].rearrange("p (c b) -> p c b", b=NB)
                        v(lambda: e.tensor_tensor(prod[:, 4 * i:4 * i + 4, :], o, ohh[:, bass.ds(g * 4, 4), :], ALU.mult), ranks[i])
                        v(lambda: e.tensor_reduce(pos[:, bass.ds(g * 4, 4)], prod[:, 4 * i:4 * i + 4, :], AX.X, ALU.add))
                v(lambda: e.tensor_copy(ti[0], pos))
                v(lambda: e.tensor_scalar(ti[1], ti[0], 127, None, ALU.bitwise_and))
                v(lambda: e.tensor_scalar(ti[2], ti[0], 7, None, ALU.logical_shift_right))
                v(lambda: e.tensor_copy(lane, ti[1]))
                v(lambda: e.tensor_copy(tile_f, ti[2]))
                ready = tv.at()
                nv = 1 + npay + (1 if wts is not None else 0)

                def move(c0, first, last, half):
                    v(lambda: e.tensor_copy(col8[:, half, :, :], packed[:, :, bass.ds(c0, 8)]), ready, chain=False, gate=True)
                    have = tv.at()
                    for j in range(8):
                        if V:
                            if j == 0:
                                wait(e, have)
                            if j % 4 == 0:
                                wait(e, (tp.sem, tp.n - 4, tp.terms))

                            def at(i):
                                return col8[:, half, i, j:j + 1]
                            e.tensor_scalar(ohl[:, j, :], iota128[:, :], at(0), None, ALU.is_equal)
                            if wts is not None:
                                e.tensor_scalar(ohlo[:, j, :], iota128b[:, :], at(2), None, ALU.is_equal)
                            for i in range(npay):
                                ins = e.tensor_scalar(oht[:, j, i * P:(i + 1) * P], iota128[:, :], at(1),
                                                      at(3 + i), ALU.is_equal, ALU.mult)
                            ins.then_inc(s_v, 1)
                        tv.inc()

                        def mm():
                            if wts is not None:
                                e.matmul(ps[:, 7, 0:NB], ohlo[:, j, :], ohh[:, bass.ds(c0 + j, 1), :].rearrange("p a b -> p (a b)"),
                                         start=first and j == 0, stop=last and j == 7)
                            return e.matmul(ps[:, 6, 0:npay * P], ohl[:, j, :], oht[:, j, 0:npay * P],
                                            start=first and j == 0, stop=last and j == 7)
                        p(mm, tv.at())

                move(0, True, False, 0)
                with lp(T // 16 - 1, (tv, 18), (tp, 16)) as c:
                    for half in range(2):
                        move(c * 16 + 8 * (half + 1), False, False, 1 - half)
                move(T - 8, False, True, 1)
                moved = tp.at()
                if wts is None:
                    v(lambda: e.tensor_copy(keys, ps[:, 6, 0:P]), moved)
                    v(lambda: e.tensor_copy(out_g[:, blk], ps[:, 6, P:2 * P]), gate=True)
                else:
                    v(lambda: e.tensor_copy(ti[0], ps[:, 6, 0:P]), moved)
                    v(lambda: e.tensor_scalar(out_g[:, blk], ti[0], 7, None, ALU.logical_shift_right))
                    v(lambda: e.tensor_scalar(ti[0], ti[0], 127, None, ALU.bitwise_and))
                    v(lambda: e.tensor_copy(ti[1], ps[:, 6, P:2 * P]))
                    v(lambda: e.tensor_scalar(ti[2], ti[1], 7, None, ALU.logical_shift_right))
                    v(lambda: e.tensor_scalar(ti[1], ti[1], 127, None, ALU.bitwise_and))
                    v(lambda: e.tensor_copy(keys, ti[2]))
                    v(lambda: e.tensor_copy(kf, ti[0]))
                    v(lambda: e.tensor_copy(gf, ti[1]))
                    v(lambda: e.scalar_tensor_tensor(kf, kf, 128.0, gf, ALU.mult, ALU.add))
                    v(lambda: e.tensor_scalar(kf, kf, sbase[:, bass.ds(s, 1)], float(E - 1), ALU.add, ALU.min))
                    v(lambda: e.tensor_copy(perm[:, blk], kf), gate=True)
                    v(lambda: e.tensor_copy(wD[:, blk], ps[:, 6, 2 * P:3 * P]), gate=True)
                    v(lambda: e.tensor_tensor(degD[:, :], degD[:, :], ps[:, 7, 0:NB], ALU.add))
                p(lambda: e.transpose(ps[:, 4, 0:P], keys, ident[:, :]), tv.at())
                v(lambda: e.tensor_copy(keyT, ps[:, 4, 0:P]), tp.at())
                p(lambda: e.matmul(ps[:, 5, 0:KP], keyT, sel, start=True, stop=True), tv.at())
                v(lambda: e.scalar_tensor_tensor(out_rel[:, kb], bmin, -128.0, ps[:, 5, 0:KP], ALU.mult, ALU.add), tp.at())

        def in_order(e, role):
            V, Q = role == "v", role == "p"
            tv, tp = Tally(s_fv), Tally(s_fp)
            tv.inc(4)

            def v(make, *marks, chain=True, gate=False):
                if V:
                    for m in marks:
                        wait(e, m)
                    if chain:
                        wait(e, tv.at())
                    if gate:
                        e.sem_inc(s_dum_v, 1)
                    make().then_inc(s_fv, 1)
                tv.inc()

            def p(make, *marks):
                if Q:
                    for m in marks:
                        wait(e, m)
                    make().then_inc(s_fp, 1)
                tp.inc()

            if V:
                e.sem_inc(s_fv, 4)
                e.sem_inc(s_fp, 4)
            tp.inc(4)
            with loop(e, SUP, (tv, 4 + T + T // 4 + 4 + 15 + 6), (tp, T + 5)) as s:
                blk, kb = bass.ds(s * T, T), bass.ds(s * KP, KP)
                v(lambda: e.tensor_scalar(ti[0], raw_d[:, blk], 7, None, ALU.logical_shift_right))
                v(lambda: e.tensor_copy(khi, ti[0]))
                v(lambda: e.tensor_scalar(ti[1], raw_d[:, blk], 127, None, ALU.bitwise_and))
                v(lambda: e.tensor_copy(klo, ti[1]))
                split = tv.at()

                def histogram(c0, first, last, half):
                    v(lambda: e.tensor_copy(col8[:, half, 0, :], khi[:, bass.ds(c0, 8)]), split, chain=False, gate=True)
                    v(lambda: e.tensor_copy(col8[:, half, 1, :], klo[:, bass.ds(c0, 8)]), chain=False)
                    have = tv.at()
                    for j in range(8):
                        if V:
                            if j == 0:
                                wait(e, have)
                            if j % 4 == 0:
                                wait(e, (tp.sem, tp.n - 4, tp.terms))
                            e.tensor_scalar(ohlo[:, j, :], iota128b[:, :], col8[:, half, 1, j:j + 1], None, ALU.is_equal)
                            e.tensor_scalar(ohh[:, j, :], iotaNb[:, :], col8[:, half, 0, j:j + 1], None, ALU.is_equal).then_inc(s_fv, 1)
                        tv.inc()
                        p(lambda: e.matmul(ps[:, 7, 0:NB], ohlo[:, j, :], ohh[:, j, :],
                                           start=first and j == 0, stop=last and j == 7), tv.at())

                histogram(0, True, False, 0)
                with loop(e, T // 16 - 1, (tv, 20), (tp, 16)) as c:
                    for half in range(2):
                        histogram(c * 16 + 8 * (half + 1), False, False, 1 - half)
                histogram(T - 8, False, True, 1)
                v(lambda: e.tensor_copy(base_, ps[:, 7, 0:NB]), tp.at())
                v(lambda: e.tensor_tensor(degD[:, :], degD[:, :], base_, ALU.add))
                p(lambda: e.matmul(ps[:, 6, 0:NB], ones_f[:, :], base_, start=True, stop=True), tv.at())
                v(lambda: e.tensor_copy(tot, ps[:, 6, 0:NB]), tp.at())
                v(lambda: e.tensor_tensor_scan(endp, ones_f[:, 0:NB], tot, 0.0, ALU.mult, ALU.add))
                step_table(e, v, p, tv, tp, 64, kb)
                v(lambda: e.tensor_copy(kf, raw_d[:, blk]), gate=True)
                p(lambda: e.matmul(ps[:, 5, 0:KP], kf, sel, start=True, stop=True), tv.at())
                v(lambda: e.tensor_copy(pays[2], raw_w[:, blk]), gate=True)
                v(lambda: e.tensor_scalar(gf, raw_s[:, blk], N - 1, None, ALU.min))
                p(lambda: e.transpose(ps[:, 4, 0:P], gf, ident[:, :]), tv.at())
                p(lambda: e.transpose(ps[:, 4, P:2 * P], pays[2], ident[:, :]), tv.at())
                v(lambda: e.scalar_tensor_tensor(relD[:, kb], bmin, -128.0, ps[:, 5, 0:KP], ALU.mult, ALU.add), tp.at())
                v(lambda: e.tensor_copy(gD[:, blk], ps[:, 4, 0:P]), gate=True)
                v(lambda: e.tensor_copy(wD[:, blk], ps[:, 4, P:2 * P]), gate=True)
            if V:
                wait(e, tv.at())
                wait(e, tp.at())
                e.sem_inc(s_v, SUP * NV_DST)
            if Q:
                wait(e, tp.at())
                e.sem_inc(s_p, SUP * NP_SORT)

        NP_SORT = 2 + 32 + T + 2
        NV_SRC = 6 + T // 8 + 3 + 32 + 6 + 8 + 7 + 64 + 5 + T + T // 8 + 2 + 2
        NV_DST = 10 + T // 8 + 3 + 32 + 6 + 8 + 7 + 64 + 5 + T + T // 8 + 14 + 2

        KT = SUP * KP
        ARR0 = 2 * NQ
        def gathers(e, layer, table, idx, with_edges):
            a0, st0 = ARR0 + layer * TILES, layer * KT
            H = T // 2

            def copy(half, s):
                cols = bass.ds(s * T + half * H, H)
                e.tensor_copy(ixb[:, half * H:(half + 1) * H], idx[:, cols]).then_inc(s_ix, 1)
                if with_edges:
                    e.tensor_copy(ixe[:, half * H:(half + 1) * H], perm[:, cols]).then_inc(s_ix, 1)

            ni = 2 if with_edges else 1
            if layer:
                e.wait_ge(s_ix, IX0[layer])
            copy(0, 0)

            def supertile(s, s_prev):
                for n in range(T // NQ):
                    e.wait_ge(s_arr, s * T + (a0 + NQ * n - NQ))
                    if s_prev is not None:
                        e.wait_ge(s_st, s_prev * KP + (st0 + (NQ * (n + 1) + NB - 1 if n < T // NQ - 1 else KP)))
                    e.sem_inc(s_dum, 1)
                    if n == 2:
                        copy(1, s)
                    if n == 2 + H // NQ:
                        copy(0, s + 1)
                    if n % (H // NQ) == 0:
                        e.wait_ge(s_ix, s * (2 * ni) + (IX0[layer] + ni * (1 + n // (H // NQ))))
                        e.sem_inc(s_dum, 1)
                    for j in range(NQ):
                        t = n * NQ + j
                        e.indirect_dma_start(M[:, t, 0:P], None, table[:, :], bass.IndirectOffsetOnAxis(ap=ixb[:, t:t + 1], axis=0))\
                            .then_inc(s_g[t % 16], 16)
                    for j in range(NQ if with_edges else 0):
                        t = n * NQ + j
                        if j % 4 == 0:
                            e.wait_ge(s_tr, s * (T // 4) + (2 * n + 1 + j // 4))
                            e.sem_inc(s_dum, 1)
                        e.indirect_dma_start(er[:, j, :], None, edge_in[:, :],
                                             bass.IndirectOffsetOnAxis(ap=ixe[:, t:t + 1], axis=0)).then_inc(s_e[t % 16], 16)

            supertile(0, None)
            if SUP > 1:
                with e.Fori(0, SUP - 1) as it:
                    supertile(it + 1, it)

        IX0 = [0] * 4
        for l in range(1, 4):
            IX0[l] = IX0[l - 1] + 2 * SUP + 1

        def arrivals(e, layer, with_edges):
            with e.Fori(0, TILES // 16) as it:
                for j in range(16):
                    e.wait_ge(s_g[j], it * 16 + 16 * (layer * (TILES // 16) + 1))
                    if with_edges:
                        e.sem_inc(s_dum_s, 1)
                        e.wait_ge(s_e[j], it * 16 + 16)
                    e.sem_inc(s_arr, 1)

        N1 = T // SG
        PB = KI - N1
        PA = T // 8 - PB
        assert 0 <= PA <= N1

        def schedule(e, group, pair=None):
            if not pair:
                with e.Fori(0, SUP) as s:
                    with e.Fori(0, N1) as m:
                        group(s, m, m * SG + SG)
                    with e.Fori(0, KI - N1) as m:
                        group(s, m + N1, T)
                return
            with e.Fori(0, PB) as i:
                pair(i, i, None)

            def supertile(s, last):
                with e.Fori(0, PA) as i:
                    pair(s * (T // 8) + (i + PB), i + PB, lambda: group(s, i, i * SG + SG))
                with e.Fori(0, N1 - PA) as i:
                    group(s, i + PA, i * SG + (PA * SG + SG))
                with e.Fori(0, PB) as i:
                    if last:
                        group(s, i + N1, T)
                    else:
                        pair(s * (T // 8) + (i + T // 8), i, lambda: group(s, i + N1, T))

            with e.Fori(0, SUP - 1) as s:
                supertile(s, False)
            with e.Fori(SUP - 1, SUP) as s:
                supertile(s, True)

        def arrivals_in_order(e):
            rows_t = edge_in[0:E // P * P, :].rearrange("(t p) f -> t p f", p=P)
            full, tail = E // P // 8, [0]

            def watch(g, half, loads):
                for h in range(2):
                    e.wait_ge(s_tr, g * 2 + (1 + h))
                    loads(h)
                for j in range(8):
                    if j % 4 == 0:
                        e.sem_inc(s_dum_s, 1)
                        if tail[0]:
                            e.wait_ge(s_etail, 16 * tail[0])
                        else:
                            e.wait_ge(s_e[j // 4], g * 16 + 16)
                    e.sem_inc(s_dum_s, 1)
                    e.wait_ge(s_g[8 * half + j], gcount(g))
                    e.sem_inc(s_arr, 1)

            def gcount(g):
                return G3 + 16 * (g // 2 + 1) if isinstance(g, int) else it_g[0] * 16 + (G3 + 16)

            G3, it_g = 3 * 16 * (TILES // 16), [None]

            def whole(g):
                def loads(h):
                    e.sem_inc(s_dum_s, 1)
                    e.dma_start(er[:, 4 * h:4 * h + 4, :], rows_t[bass.ds(g * 8 + 4 * h, 4), :, :].rearrange("t p f -> p t f"))\
                        .then_inc(s_e[h], 16)
                return loads

            def ragged(g):
                def loads(h):
                    for j in range(4):
                        t = g * 8 + 4 * h + j
                        n = min(P, max(0, E - t * P))
                        if n:
                            e.dma_start(er[0:n, 4 * h + j, :], edge_in[t * P:t * P + n, :]).then_inc(s_etail, 16)
                            tail[0] += 1
                return loads

            with e.Fori(0, full // 2) as it:
                it_g[0] = it
                for half in range(2):
                    g = it * 2 + half
                    watch(g, half, whole(g))
            if full % 2:
                watch(full - 1, 0, whole(full - 1))
            for g in range(full, TILES // 8):
                watch(g, g % 2, ragged(g))

        def steps_pe(e, layer, row, regs, ready, r0, width, pair=None):
            def group(s, m, need):
                k0 = s * KP + m * SG
                e.load(regs, tab[row:row + 1, bass.ds(k0, SG)])
                tau_v = [e.snap(r, min_val=0, max_val=T - 1) for r in regs]
                e.wait_ge(ready, s * T + need + r0)
                for q in range(SG // 3):
                    e.wait_ge(s_oh, k0 + (layer * (KT + SG) + 3 * q + 3))
                    for i in range(3):
                        j = 3 * q + i
                        e.matmul(ps[:, q, i * W1C:i * W1C + width], oh[:, j, :],
                                 M[:, bass.ds(tau_v[j], 1), 0:width].rearrange("p a f -> p (a f)"),
                                 start=True, stop=True).then_inc(s_st, 1)

            schedule(e, group, pair)

        def steps_dve(e, layer, rel, row, regs, width, pair=None):
            def onehot(j, k):
                e.tensor_scalar(oh[:, j, :], iota128[:, :], k, None, ALU.is_equal).then_inc(s_oh, 1)

            for j in range(SG):
                onehot(j, rel[:, j:j + 1])

            def group(s, m, need):
                k0 = s * KP + m * SG
                e.load(regs, tab[row + 32:row + 33, bass.ds(k0, SG)])
                b = [e.snap(r, min_val=0, max_val=NB - 1) for r in regs]
                e.wait_ge(s_oh, k0 + (layer * (KT + SG) + SG))
                e.sem_inc(s_dum_v, 1)
                e.tensor_copy(relc[:, :], rel[:, bass.ds(k0 + SG, SG)]).then_inc(s_rc, 1)
                for q in range(SG // 3):
                    e.wait_ge(s_st, k0 + (layer * KT + 3 * q + 3))
                    for i in range(3):
                        j = 3 * q + i
                        e.wait_ge(s_add, k0 + (layer * KT + j + 1))
                        a = acc[:, bass.ds(b[j], 1), 0:width].rearrange("p a f -> p (a f)")
                        e.tensor_tensor(a, a, ps[:, q, i * W1C:i * W1C + width], ALU.add).then_inc(s_add, 1)
                        if j == 0:
                            e.wait_ge(s_rc, s * KI + m + (layer * SUP * KI + 1))
                        onehot(j, relc[:, j:j + 1])

            schedule(e, group, pair)

        def rows(ap, g, k=NG):
            return ap[0:ap.shape[0] // P * P, :].rearrange("(i p) f -> i p f", p=P)[bass.ds(g * NG, k), :, :].rearrange("i p f -> p i f")

        n3 = lambda ap: ap.rearrange("p (i f) -> p i f", f=P)
        SRC_X, DST_X = [x_in, x1, x2, x3], [x1, x2, x3, None]

        def node(e, role, layer, tl, tsx, tv, tp, ta):
            V, Q, A, S = role == "v", role == "p", role == "a", role == "s"

            def op(mine, sm, tally, make, marks, chain, gate=False):
                if mine:
                    for m in marks:
                        wait(e, m)
                    if chain:
                        wait(e, tally.at())
                    if gate:
                        e.sem_inc(s_dum_v, 1)
                    make().then_inc(sm, 1)
                tally.inc()

            v = lambda make, *marks, gate=False: op(V, s_nv, tv, make, marks, True, gate)
            p = lambda make, *marks: op(Q, s_np, tp, make, marks, False)
            a = lambda make, *marks: op(A, s_na, ta, make, marks, True)
            pf = lambda b, nb_: ps[:, b:b + nb_, :]
            banks = -(-NG // GA)

            def parts(k=NG):
                return [(b, b * GA, min(GA, NG - b * GA)) for b in range(banks)]

            def psn(b0):
                return [(ps[:, b0 + b, 0:n * P], i0 * P, n * P) for b, i0, n in parts()]

            def transpose_to(b0, src_, dst_, mark):
                def tr():
                    for i in range(NG):
                        o = ps[:, b0 + i // GA, (i % GA) * P:(i % GA) * P + P]
                        ins = e.transpose(o, src_[:, i * P:(i + 1) * P], ident[:, :])
                    return ins
                p(tr, mark)
                done = tp.at()

                def cp():
                    for o, c0, n in psn(b0):
                        ins = e.activation(dst_[:, c0:c0 + n], o, ACT.Copy)
                    return ins
                a(cp, done)

            xs, xd = SRC_X[layer], DST_X[layer]

            def body(g, last):
                full = NG - 1 if last else NG
                if S:
                    wait(e, tv.at())
                    e.sem_inc(s_dum_s, 1)
                    if last and layer == 0:
                        if full:
                            e.dma_start(n3(nxg)[:, 0:full, :], rows(xs, g, full)).then_inc(s_nl, 16)
                        else:
                            e.dma_start(n3(nxg)[0:LASTN, NG - 1, :], xs[(NB - 1) * P:N, :]).then_inc(s_nl, 16)
                        e.dma_start(n3(nxg)[0:LASTN, NG - 1, :], xs[(NB - 1) * P:N, :]).then_inc(s_nl, 16)
                    else:
                        e.dma_start(n3(nxg), rows(xs, g)).then_inc(s_nl, 16)
                tl.inc(32 if last and layer == 0 else 16)
                loaded = tl.at()
                ab = acc[:, bass.ds(g * NG, NG), :] if V else None
                if layer == 0:
                    dg = nst[:, 0:NG]
                    v(lambda: e.tensor_scalar(dg, ab[:, :, P:P + 1].rearrange("p a b -> p (a b)"), 1.0, None, ALU.max), loaded)
                    v(lambda: e.reciprocal(dg, dg))

                    def mean():
                        for i in range(NG):
                            ins = e.tensor_scalar(nag[:, i * P:(i + 1) * P], ab[:, i:i + 1, 0:P].rearrange("p a b -> p (a b)"), dg[:, i:i + 1], None, ALU.mult)
                        return ins
                    v(mean)
                    up = tv.at()
                    transpose_to(0, nxg, nxT, up)
                    transpose_to(2, nag, naT, up)
                    ready = ta.at()

                    def mm():
                        for i in range(NG):
                            o = ps[:, 4 + i // GA, (i % GA) * P:(i % GA) * P + P]
                            c = slice(i * P, (i + 1) * P)
                            e.matmul(o, nxT[:, c], wua_sb[:, :], start=True, stop=False)
                            ins = e.matmul(o, naT[:, c], wtu_sb[:, :], start=False, stop=True)
                        return ins
                    p(mm, ready)
                    done = tp.at()

                    def addb():
                        for o, c0, n in psn(4):
                            ins = e.tensor_tensor(n3(nh2[:, c0:c0 + n]), n3(o), bias[:, 0:1, :].to_broadcast([P, n // P, P]), ALU.add)
                        return ins
                    v(addb, done)
                    v(lambda: e.scalar_tensor_tensor(nz, nh2, 0.0, nxg, ALU.max, ALU.add))
                elif layer == 1:
                    dis = degD[:, bass.ds(g * NG, NG)] if V else None

                    def agg():
                        for i in range(NG):
                            ins = e.tensor_scalar(nag[:, i * P:(i + 1) * P], ab[:, i:i + 1, 0:P].rearrange("p a b -> p (a b)"), dis[:, i:i + 1], None, ALU.mult)
                        return ins
                    v(agg, loaded)
                    v(lambda: e.scalar_tensor_tensor(nag, nxg, eps_sb[:, 0:1], nag, ALU.mult, ALU.add))
                    v(lambda: e.tensor_tensor(nz, nag, nxg, ALU.add))
                elif layer in (2, 3):
                    v(lambda: e.scalar_tensor_tensor(n3(nag), n3(nxg), eps_sb[:, layer - 1:layer], ab[:, :, 0:P], ALU.mult, ALU.add), loaded)
                    transpose_to(0, nag, naT, tv.at())
                    nh = 1 if layer == 2 else HID // P
                    for h in range(nh):
                        wm = w21_sb[:, :] if layer == 2 else w31_sb[:, h * P:(h + 1) * P]
                        bc = b21c[:, 0:1] if layer == 2 else b31c[:, h:h + 1]
                        b0 = 2 + 2 * (h % 2)

                        def up_():
                            for o, c0, n in psn(b0):
                                ins = e.matmul(o, wm, naT[:, c0:c0 + n], start=True, stop=True)
                            return ins
                        p(up_, ta.at())

                        def relu():
                            for o, c0, n in psn(b0):
                                ins = e.activation(nhT[:, h * NW + c0:h * NW + c0 + n], o, ACT.Relu, bias=bc)
                            return ins
                        a(relu, tp.at())

                    def down():
                        for i in range(NG):
                            o = ps[:, 6 + i // GA, (i % GA) * P:(i % GA) * P + P]
                            for h in range(nh):
                                wm = w22_sb[:, :] if layer == 2 else w32_sb[:, h, :]
                                ins = e.matmul(o, nhT[:, h * NW + i * P:h * NW + (i + 1) * P], wm, start=h == 0, stop=h == nh - 1)
                        return ins
                    p(down, ta.at())
                    done = tp.at()
                    br = 1 if layer == 2 else 2

                    def addb():
                        for o, c0, n in psn(6):
                            ins = e.tensor_tensor(n3(nh2[:, c0:c0 + n]), n3(o), bias[:, br:br + 1, :].to_broadcast([P, n // P, P]), ALU.add)
                        return ins
                    v(addb, done)
                    v(lambda: e.tensor_tensor(nz, nh2, nxg, ALU.add))

                def stats():
                    for i in range(NG):
                        ins = e.bn_stats(nst[:, i * 6:(i + 1) * 6], nz[:, i * P:(i + 1) * P])
                    return ins
                v(stats)

                def aggr():
                    for i in range(NG):
                        ins = e.bn_aggr(nmv[:, 2 * i:2 * i + 2], nst[:, i * 6:(i + 1) * 6])
                    return ins
                v(aggr, gate=True)
                mv = nmv.rearrange("p (i c) -> p i c", c=2)
                a(lambda: e.activation(nrs[:, 0:NG], mv[:, :, 1:2].rearrange("p a b -> p (a b)"), ACT.Sqrt, bias=eps_sb[:, 3:4]), tv.at())
                v(lambda: e.reciprocal(nrs[:, NG:2 * NG], nrs[:, 0:NG]), ta.at())
                stored = tsx.at()

                def norm():
                    for i in range(NG):
                        ins = e.tensor_scalar(nout[:, i * P:(i + 1) * P], nz[:, i * P:(i + 1) * P], nmv[:, 2 * i:2 * i + 1],
                                              nrs[:, NG + i:NG + i + 1], ALU.subtract, ALU.mult)
                    return ins
                v(norm, stored)
                nd = 1
                if layer == 0:
                    dis = degD[:, bass.ds(g * NG, NG)] if V else None

                    def scale():
                        for i in range(NG):
                            ins = e.tensor_scalar(nag[:, i * P:(i + 1) * P], nout[:, i * P:(i + 1) * P], dis[:, i:i + 1], None, ALU.mult)
                        return ins
                    v(scale)
                    nd = 2
                elif layer == 2:
                    v(lambda: e.tensor_tensor(n3(nag), n3(nout), bias[:, 3:4, :].to_broadcast([P, NG, P]), ALU.add))
                    nd = 2
                if S:
                    wait(e, tv.at())
                    e.sem_inc(s_dum_s, 1)
                    if layer == 3 and last:
                        if full:
                            e.dma_start(rows(out, g, full), n3(nout)[:, 0:full, :]).then_inc(s_ns, 16)
                        else:
                            e.dma_start(out[(NB - 1) * P:N, :], n3(nout)[0:LASTN, NG - 1, :]).then_inc(s_ns, 16)
                        e.dma_start(out[(NB - 1) * P:N, :], n3(nout)[0:LASTN, NG - 1, :]).then_inc(s_ns, 16)
                    else:
                        e.dma_start(rows(out if layer == 3 else xd, g), n3(nout)).then_inc(s_ns, 16)
                        if nd == 2:
                            e.dma_start(rows(t1 if layer == 0 else t3, g), n3(nag)).then_inc(s_ns, 16)
                tsx.inc(32 if (layer == 3 and last) else 16 * nd)
                if nd == 2:
                    v(lambda: e.memset(nrs[:, 0:1], 0.0), tsx.at())

            if layer == 0:
                v(lambda: e.memset(nxg, 0.0), *([(s_st, KT, ())] if V else []))
            per = NODE_PER[layer]
            special = layer in (0, 3)
            trips = GROUPS - 1 if special else GROUPS
            if trips:
                with loop(e, trips, (tl, 16), (tsx, per[0]), (tv, per[1]), (tp, per[2]), (ta, per[3])) as g:
                    body(g, False)
            if special:
                body(GROUPS - 1, True)

        NODE_PER = [(32, 11, 3, 3), (16, 7, 0, 1), (32, 9, 3, 3), (16, 7, 6, 6)]

        U0 = 3 * TILES + ARR0
        MV0 = 8

        def edge_pe(e):
            def pair(pi, loc, then):
                for h in range(2):
                    e.wait_ge(s_arr, pi * 8 + (U0 + 4 * h + 4))
                    e.wait_ge(s_et, pi * 2 + (h + 1))
                    for j in range(4):
                        ins = e.transpose(ps[:, 4, j * P:(j + 1) * P], er[:, 4 * h + j, :], ident[:, :])
                    ins.then_inc(s_tr, 1)
                    e.wait_ge(s_et, pi * 2 + (h + 2))
                    e.wait_ge(s_vv, pi * 2 + (h + 1))
                    for j in range(4):
                        ins = e.matmul(ps[:, 5 + h, j * P:(j + 1) * P], et[:, h, j * P:(j + 1) * P], we_sb[:, :],
                                       start=True, stop=True)
                    ins.then_inc(s_u, 1)
                if then:
                    then()
            return pair

        def edge_act(e):
            def pair(pi, loc, then):
                for h in range(2):
                    e.wait_ge(s_tr, pi * 2 + (h + 3))
                    e.activation(et[:, h, :], ps[:, 4, :], ACT.Copy).then_inc(s_et, 1)
                e.wait_ge(s_c, pi * 2 + 2)
                e.activation(eb2, eb2, ACT.Exp).then_inc(s_ex, 1)
                e.wait_ge(s_ex, pi * 3 + 1)
                e.activation(eb2, eb2, ACT.Ln, bias=1.0).then_inc(s_ex, 1)
                e.wait_ge(s_ex, pi * 3 + 2)
                e.activation(eb2, eb2, ACT.Tanh).then_inc(s_ex, 1)
            return pair

        def edge_dve(e):
            def pair(pi, loc, then):
                def m_at(h):
                    return M[:, bass.ds(loc * 8 + 4 * h, 4), 0:P]
                n4 = lambda ap: ap.rearrange("p (t f) -> p t f", f=P)
                for h in range(2):
                    e.wait_ge(s_mv, pi * 8 + (MV0 - 4 + 4 * h))
                    e.wait_ge(s_u, pi * 2 + (h + 1))
                    e.tensor_tensor(n4(vb[:, h, :]), m_at(h), n4(ps[:, 5 + h, :]), ALU.add).then_inc(s_vv, 1)
                for h in range(2):
                    e.wait_ge(s_vv, pi * 2 + (h + 3))
                    e.tensor_scalar(eb[:, h, :], vb[:, h, :], 20.0, None, ALU.min).then_inc(s_c, 1)
                if then:
                    then()
                e.wait_ge(s_ex, pi * 3 + 3)
                for h in range(2):
                    e.tensor_tensor(m_at(h), n4(eb[:, h, :]), n4(vb[:, h, :]), ALU.mult).then_inc(s_mv, 4)
            return pair

        F, rem = E // SE, E % SE
        r_full, r_tail = rem // T, rem % T

        def node_tallies():
            return [Tally(s) for s in (s_nl, s_ns, s_nv, s_np, s_na)]


        def bcast_row(ap, n):
            return ap.rearrange("(a n) -> a n", a=1).to_broadcast([P, n])

        def raw_views(dst, src):
            if F:
                yield dst[:, 0:F * T].rearrange("p (s c) -> p s c", c=T), src[0:F * SE].rearrange("(s p c) -> p s c", p=P, c=T)
            if r_full:
                yield dst[0:r_full, F * T:TILES], src[F * SE:F * SE + r_full * T].rearrange("(p c) -> p c", c=T)
            if r_tail:
                yield dst[r_full:r_full + 1, F * T:F * T + r_tail], src[F * SE + r_full * T:E].rearrange("(p c) -> p c", p=1)

        weight_loads = [
            (wt_sb, Wt), (wua_sb[:, :], Wu[0:P, :]), (wub_sb, Wu[P:2 * P, :]), (w21_sb[:, :], W21), (w22_sb[:, :], W22),
            (we_sb[:, :], We), (w31_sb[:, :], W31[0:P, :]), (w31g_sb, W31[P:2 * P, :]),
            (w32_sb[:, :, :], W32.rearrange("(h p) n -> p h n", p=P)),
            (bias[:, 0, :], bcast_row(bu, P)), (bias[:, 1, :], bcast_row(b22, P)), (bias[:, 2, :], bcast_row(b32, P)),
            (bias[:, 3, :], bcast_row(be, P)),
            (eps_sb[:, 0:1], bcast_row(eps1, 1)), (eps_sb[:, 1:2], bcast_row(eps2, 1)),
            (eps_sb[:, 2:3], eps3.to_broadcast([P, 1])),
            (b21c[:, :], b21.rearrange("(p a) -> p a", a=1)), (globc[:, :], glob.rearrange("a p -> p a")),
            (b31c[:, :], b31.rearrange("(h p) -> p h", p=P)),
        ]
        e1 = E - 1
        r1, t1_ = (e1 % SE) // T, (e1 % SE) % T
        assert e1 // SE == F and r_full == r1 and t1_ + 1 == r_tail and t1_ > 0

        def shifted_views():
            src = dst_in
            yield next_d[:, 0:F * T].rearrange("p (s c) -> p s c", c=T), src[1:F * SE + 1].rearrange("(s p c) -> p s c", p=P, c=T)
            yield next_d[0:r1, F * T:TILES], src[F * SE + 1:F * SE + 1 + r1 * T].rearrange("(p c) -> p c", c=T)
            yield next_d[r1:r1 + 1, F * T:F * T + t1_], src[F * SE + 1 + r1 * T:E].rearrange("(p c) -> p c", p=1)

        raw_loads = [v for d, s_ in ((raw_s, src_in), (raw_d, dst_in), (raw_w, w_in.rearrange("e a -> (e a)"))) for v in raw_views(d, s_)] + list(shifted_views())
        NLD = 16 * (len(weight_loads) + len(raw_loads))
        NCST, TABLES = 22, [x_in, t1, x2, t3]
        SQ_AT = 7 + SUP * (NV_SRC + NV_DST) + 3 + 3
        NS_DONE = [32 * GROUPS, 48 * GROUPS, 80 * GROUPS]

        block = ctx.enter_context(nc.Block())

        @block.sync
        def _(e):
            e.wait_ge(s_cst, 4)
            n_node = node_tallies()
            for d, s_ in weight_loads + raw_loads:
                e.dma_start(d, s_).then_inc(s_ld, 16)
            for layer in range(4):
                if layer < 3:
                    arrivals(e, layer, False)
                else:
                    with e.If(e.value_load(unsorted[0:1, 0:1], min_val=0, max_val=P) == 0):
                        arrivals_in_order(e)
                    with e.Else():
                        arrivals(e, layer, True)
                e.wait_ge(s_st, (layer + 1) * KT)
                node(e, "s", layer, *n_node)
            e.wait_ge(s_ns, n_node[1].n)

        @block.gpsimd
        def _(e):
            for s_, k in ((s_arr, ARR0), (s_tr, 2), (s_et, 1), (s_vv, 2), (s_add, 1)):
                e.sem_inc(s_, k)
            e.memset(raw_s[:, F * T:TILES] if rem else raw_s[:, 0:1], NB * P - 1).then_inc(s_cst, 1)
            e.memset(raw_d[:, F * T:TILES] if rem else raw_d[:, 0:1], NB * P - 1).then_inc(s_cst, 1)
            e.memset(raw_w[:, F * T:TILES] if rem else raw_w[:, 0:1], 0.0).then_inc(s_cst, 1)
            e.memset(next_d[:, F * T:TILES], NB * P - 1).then_inc(s_cst, 1)
            c = [4]

            def k(ins):
                ins.then_inc(s_cst, 1)
                c[0] += 1

            k(e.memset(ident[:, :], 0.0))
            k(e.memset(ones_f[:, :], 1.0))
            k(e.memset(ones_b[:, :], 1.0))
            k(e.memset(ltri[:, :], 1.0))
            k(e.memset(bigcol[:, :], 0.0))
            k(e.memset(degD[:, :], 0.0))
            k(e.memset(gS[:, TILES:TILES + T // 2], 0))
            k(e.memset(gD[:, TILES:TILES + T // 2], 0))
            k(e.memset(perm[:, TILES:TILES + T // 2], 0))
            k(e.memset(eps_sb[:, 3:4], LN_EPS))
            k(e.memset(relS[:, SUP * KP:SUP * KP + SG], -1.0))
            k(e.memset(relD[:, SUP * KP:SUP * KP + SG], -1.0))
            it_ = dict(allow_small_or_imprecise_dtypes=True)
            k(e.iota(iota128[:, :], [[1, P]], base=0, channel_multiplier=0, **it_))
            k(e.iota(iotaK[:, :], [[1, KP]], base=0, channel_multiplier=0, **it_))
            k(e.iota(iota_p[:, :], [[0, 1]], base=0, channel_multiplier=1, **it_))
            k(e.iota(neg128p[:, :], [[0, 1]], base=0, channel_multiplier=-P, **it_))
            k(e.iota(sbase[:, :], [[SE, SUP]], base=0, channel_multiplier=0, **it_))
            e.wait_ge(s_cst, c[0])
            k(e.affine_select(out=ident[:, :], in_=ident[:, :], compare_op=ALU.not_equal, fill=1.0, base=0,
                              pattern=[[-1, P]], channel_multiplier=1))
            k(e.affine_select(out=ltri[:, :], in_=ltri[:, :], compare_op=ALU.is_ge, fill=0.0, base=-1,
                              pattern=[[1, P]], channel_multiplier=-1))
            k(e.affine_select(out=bigcol[:, :], in_=bigcol[:, :], compare_op=ALU.is_ge, fill=1e6, base=NB - 1,
                              pattern=[[0, 1]], channel_multiplier=-1))
            assert c[0] == NCST + 2, c[0]
            for layer in range(4):
                e.wait_ge(s_mv, layer + 1)
                if layer < 3:
                    gathers(e, layer, TABLES[layer], gS if layer < 2 else gD, False)
                else:
                    with e.If(e.value_load(unsorted[0:1, 0:1], min_val=0, max_val=P) == 0):
                        gathers(e, layer, TABLES[layer], gD, False)
                    with e.Else():
                        gathers(e, layer, TABLES[layer], gD, True)

        @block.vector
        def _(e):
            tv, tp = Tally(s_v), Tally(s_p)
            e.wait_ge(s_cst, NCST + 2)
            e.wait_ge(s_ld, NLD)

            def v(make, *marks):
                for m in marks:
                    wait(e, m)
                if tv.n:
                    wait(e, tv.at())
                make().then_inc(s_v, 1)
                tv.inc()

            v(lambda: e.tensor_copy(iotaNb[:, :], iota128[:, 0:NB]))
            v(lambda: e.tensor_copy(iota128b[:, :], iota128[:, :]))
            v(lambda: e.memset(packed, 0.0))
            v(lambda: e.tensor_scalar(eps_sb[:, 0:3], eps_sb[:, 0:3], 1.0, None, ALU.add))
            tp.inc()
            v(lambda: e.tensor_copy(keys, ps[:, 0, 0:P]), tp.at())
            tp.inc()
            v(lambda: e.tensor_copy(wtu_sb[:, :], ps[:, 1, 0:P]), tp.at())
            v(lambda: e.tensor_tensor(b31c[:, :], b31c[:, :], ps[:, 1, P:P + HID // P], ALU.add))
            sort(e, "v", tv, tp, raw_s, raw_d, None, relS, gS, 0)
            after = ohh_flat[:, 0:TILES]
            v(lambda: e.tensor_tensor(after, raw_d, next_d, ALU.is_gt))
            v(lambda: e.tensor_reduce(lcol[:, 0:1], after, AX.X, ALU.max))
            tp.inc()
            v(lambda: e.tensor_copy(unsorted[:, :], ps[:, 7, 0:1]), tp.at())
            e.wait_ge(s_v, tv.n)
            with e.If(e.value_load(unsorted[0:1, 0:1], min_val=0, max_val=P) == 0):
                in_order(e, "v")
            with e.Else():
                sort(e, "v", tv, tp, raw_d, raw_s, raw_w, relD, gD, 64)
            v(lambda: e.tensor_scalar(degm[:, :], degD[:, :], 0.5, None, ALU.is_gt))
            v(lambda: e.tensor_scalar(degD[:, :], degD[:, :], 1.0, None, ALU.max))
            v(lambda: e.reciprocal(degD[:, :], degD[:, :]))
            assert tv.n == SQ_AT, tv.n
            e.wait_ge(s_a, 1)
            v(lambda: e.tensor_tensor(degD[:, :], degD[:, :], degm[:, :], ALU.mult))
            regs = [e.alloc_register(f"node_tile{j}") for j in range(SG)]
            n_node = node_tallies()
            for layer in range(4):
                v(lambda: e.memset(acc_flat, 0.0))
                if layer == 0:
                    v(lambda: e.memset(M[:, :, P:W1C], 1.0))
                e.wait_ge(s_v, tv.n)
                if layer:
                    e.wait_ge(s_ns, NS_DONE[layer - 1])
                e.sem_inc(s_mv, 1 if layer < 3 else MV0 - 3)
                steps_dve(e, layer, relS if layer < 2 else relD, 0 if layer < 2 else 64, regs, W1C if layer == 0 else P,
                          edge_dve(e) if layer == 3 else None)
                e.wait_ge(s_add, (layer + 1) * KT + 1)
                node(e, "v", layer, *n_node)
                e.wait_ge(s_nv, n_node[2].n)

        @block.tensor
        def _(e):
            tv, tp = Tally(s_v), Tally(s_p)
            e.wait_ge(s_cst, NCST + 2)
            e.wait_ge(s_ld, NLD)
            e.transpose(ps[:, 0, 0:P], wt_sb, ident[:, :]).then_inc(s_p, 1)
            tv.inc(5)
            wait(e, tv.at())
            e.matmul(ps[:, 1, 0:P], keys, wub_sb, start=True, stop=True)
            for h in range(HID // P):
                ins = e.matmul(ps[:, 1, P + h:P + h + 1], w31g_sb[:, h * P:(h + 1) * P], globc[:, :], start=True, stop=True)
            ins.then_inc(s_p, 1)
            tp.inc(2)
            tv.inc(2)
            sort(e, "p", tv, tp, raw_s, raw_d, None, relS, gS, 0)
            tv.inc(2)
            wait(e, tv.at())
            e.matmul(ps[:, 7, 0:1], ones_f[:, :], lcol[:, 0:1], start=True, stop=True).then_inc(s_p, 1)
            tp.inc()
            tv.inc()
            wait(e, tv.at())
            with e.If(e.value_load(unsorted[0:1, 0:1], min_val=0, max_val=P) == 0):
                e.wait_ge(s_fp, 4)
                in_order(e, "p")
            with e.Else():
                sort(e, "p", tv, tp, raw_d, raw_s, raw_w, relD, gD, 64)
            regs = [e.alloc_register(f"edge_tile{j}") for j in range(SG)]
            n_node = node_tallies()
            for layer in range(4):
                ready, r0 = ((s_arr, ARR0), (s_arr, ARR0 + TILES), (s_m, 0), (s_mv, MV0))[layer]
                steps_pe(e, layer, 0 if layer < 2 else 64, regs, ready, r0, W1C if layer == 0 else P,
                         edge_pe(e) if layer == 3 else None)
                node(e, "p", layer, *n_node)

        @block.scalar
        def _(e):
            e.wait_ge(s_v, SQ_AT)
            n_node = node_tallies()
            e.activation(degD[:, :], degD[:, :], ACT.Sqrt).then_inc(s_a, 1)
            for layer in range(4):
                if layer == 2:
                    with e.Fori(0, SUP) as s:
                        with e.Fori(0, T) as t:
                            e.wait_ge(s_arr, s * T + t + (ARR0 + 2 * TILES + 1))
                            e.sem_inc(s_dum_a, 1)
                            m = M[:, bass.ds(t, 1), 0:P].rearrange("p a f -> p (a f)")
                            e.activation(m, m, ACT.Copy, scale=wD[:, bass.ds(s * T + t, 1)]).then_inc(s_m, 1)
                if layer == 3:
                    schedule(e, lambda s, m, need: None, edge_act(e))
                node(e, "a", layer, *n_node)


_INS = ["x", "src", "dst", "edge_attr_128", "edge_weight1", "L0_gnn_W_t", "L0_gnn_W_u", "L0_gnn_b_u", "L1_gnn_eps",
        "L2_gnn_eps", "L2_gnn_W1", "L2_gnn_b1", "L2_gnn_W2", "L2_gnn_b2", "L3_gnn_globals_g", "L3_gnn_W_e_k",
        "L3_gnn_W_e_b", "L3_gnn_eps", "L3_gnn_W1", "L3_gnn_b1", "L3_gnn_W2", "L3_gnn_b2"]


def kernel(**inputs):
    import numpy as _np
    import concourse.bacc as _bacc
    from concourse import mybir as _mybir
    from concourse.bass_utils import run_bass_kernel_spmd as _run

    nc = _bacc.Bacc("TRN2", target_bir_lowering=False, num_devices=1)
    arrays, args = {}, []
    for name in _INS:
        a = _np.ascontiguousarray(inputs[name])
        arrays[f"in_{name}"] = a
        args.append(nc.dram_tensor(f"in_{name}", a.shape, _mybir.dt.from_np(a.dtype), kind="ExternalInput").ap())
    args.append(nc.dram_tensor("out_x", inputs["x"].shape, _mybir.dt.float32, kind="ExternalOutput").ap())
    graph_layers(nc, *args)
    return _run(nc, [arrays], core_ids=[0]).results[0]["out_x"]
```
